# Optimizing a Trainium2 kernel written in Bass

```python
import numpy as np
import jax
import jax.numpy as jnp

def _softmax(x, axis=-1):
    return jax.nn.softmax(x, axis=axis)

def _gelu(x):
    return jax.nn.gelu(x, approximate=True)

def _silu(x):
    return jax.nn.silu(x)

def _sigmoid(x):
    return jax.nn.sigmoid(x)

def _layernorm(x, axis=-1, eps=1e-05):
    m = jnp.mean(x, axis=axis, keepdims=True)
    v = jnp.var(x, axis=axis, keepdims=True)
    return (x - m) / jnp.sqrt(v + eps)

def _scatter_add(tgt, idx, src, axis=0):
    return tgt.at[idx].add(src)

def _segment_sum(src, seg, n):
    return jax.ops.segment_sum(src, seg, n)
kernel_name = 'mk_adaln_d2_jaxref_r8_0e26ff'

def setup_inputs(seed: int=0):
    np.random.seed(seed)
    _w = jnp.asarray

    def _L0_attn_setup():
        import jax, jax.numpy as jnp
        import numpy as np
        D_MODEL = 128
        D_STATE = 16
        D_CONV = 4
        EXPAND = 2
        E = EXPAND * D_MODEL
        B, L = (4, 512)
        key = jax.random.key(seed)
        ks = jax.random.split(key, 8)
        x = jax.random.normal(ks[0], (B, L, D_MODEL), dtype=jnp.float32)
        W_in = jax.random.normal(ks[1], (D_MODEL, 2 * E), dtype=jnp.float32) * 0.02
        b_in = jnp.zeros((2 * E,), dtype=jnp.float32)
        conv_w = jax.random.normal(ks[2], (E, 1, D_CONV), dtype=jnp.float32) * 0.1
        conv_b = jnp.zeros((E,), dtype=jnp.float32)
        A = jax.random.normal(ks[3], (E, D_STATE), dtype=jnp.float32) * 0.01
        C = jax.random.normal(ks[4], (E, D_STATE), dtype=jnp.float32) * 0.01
        Dp = jnp.ones((E,), dtype=jnp.float32) * 0.01
        W_out = jax.random.normal(ks[5], (E, D_MODEL), dtype=jnp.float32) * 0.02
        b_out = jnp.zeros((D_MODEL,), dtype=jnp.float32)
        return {'x': x, 'W_in': W_in, 'b_in': b_in, 'conv_w': conv_w, 'conv_b': conv_b, 'A': A, 'C': C, 'Dp': Dp, 'W_out': W_out, 'b_out': b_out}
    _L0_attn_in = _L0_attn_setup()

    def _L0_ffn_setup():
        import jax, jax.numpy as jnp
        import numpy as np
        B, T, C = (2, 256, 128)
        H, D = (16, 64)
        CR = 8
        R = C // CR
        ROPE = D // 2
        NOPE = D - ROPE
        E, K, I, S = (8, 2, 64, 1)
        THETA = 100000.0
        EPS = 1e-05

        def _rmsnorm(x, w):
            rms = jnp.sqrt(jnp.mean(x * x, axis=-1, keepdims=True) + EPS)
            return w * (x / rms)

        def _rope(xh):
            d = xh.shape[-1]
            t = jnp.arange(xh.shape[2], dtype=jnp.float32)
            freqs = 1.0 / THETA ** (jnp.arange(0, d, 2, dtype=jnp.float32) / d)
            ang = jnp.outer(t, freqs)
            cos, sin = (jnp.cos(ang), jnp.sin(ang))
            xr = xh.reshape(xh.shape[:-1] + (d // 2, 2))
            x0, x1 = (xr[..., 0], xr[..., 1])
            rot = jnp.stack([x0 * cos - x1 * sin, x0 * sin + x1 * cos], axis=-1)
            return rot.reshape(xh.shape)

        def _attention(x, Wq, Wkva, Wkvb, Wo):
            b, t, _ = x.shape
            q = (x @ Wq).reshape(b, t, H, D).transpose(0, 2, 1, 3)
            ckv = x @ Wkva
            kv_latent, k_rope = (ckv[:, :, :R], ckv[:, :, R:])
            kv = (kv_latent @ Wkvb).reshape(b, t, H, NOPE).transpose(0, 2, 1, 3)
            k_rope = jnp.broadcast_to(k_rope[:, None, :, :], (b, H, t, ROPE))
            q_nope, q_rope = (q[..., :NOPE], q[..., NOPE:])
            q = jnp.concatenate([q_nope, _rope(q_rope)], axis=-1)
            k = jnp.concatenate([kv, _rope(k_rope)], axis=-1)
            v = jnp.concatenate([kv, jnp.zeros_like(k_rope)], axis=-1)
            att = jnp.einsum('bhqd,bhkd->bhqk', q, k) / jnp.sqrt(jnp.float32(D))
            mask = jnp.tril(jnp.ones((t, t), dtype=bool))
            att = jnp.where(mask, att, jnp.float32(-jnp.inf))
            att = jax.nn.softmax(att, axis=-1)
            y = jnp.einsum('bhqk,bhkd->bhqd', att, v)
            y = y.transpose(0, 2, 1, 3).reshape(b, t, H * D)
            return y @ Wo

        def _experts(x_flat, Wg, Wu, Wd):
            g = jax.nn.silu(jnp.einsum('nc,eci->nei', x_flat, Wg))
            u = jnp.einsum('nc,eci->nei', x_flat, Wu)
            return jnp.einsum('nei,eic->nec', g * u, Wd)

        def _moe(x, Wgate, expert_bias, Wg, Wu, Wd, sWg, sWu, sWd):
            b, t, c = x.shape
            xf = x.reshape(-1, c)
            shared = jnp.mean(_experts(xf, sWg, sWu, sWd), axis=1)
            logits = xf @ Wgate + expert_bias
            probs = jax.nn.softmax(logits, axis=-1)
            topk_p, topk_i = jax.lax.top_k(probs, K)
            topk_p = topk_p / jnp.sum(topk_p, axis=-1, keepdims=True)
            comb = jnp.sum(jax.nn.one_hot(topk_i, E, dtype=xf.dtype) * topk_p[..., None], axis=1)
            routed = jnp.einsum('ne,nec->nc', comb, _experts(xf, Wg, Wu, Wd))
            return (shared + routed).reshape(b, t, c)
        key = jax.random.key(seed)
        ks = jax.random.split(key, 16)
        w = lambda k, shp: jax.random.normal(k, shp, dtype=jnp.float32) * 0.02
        return {'x': jax.random.normal(ks[0], (B, T, C), dtype=jnp.float32), 'w_ln1': jnp.ones((C,), jnp.float32), 'Wq': w(ks[1], (C, H * D)), 'Wkva': w(ks[2], (C, R + ROPE)), 'Wkvb': w(ks[3], (R, H * NOPE)), 'Wo': w(ks[4], (H * D, C)), 'w_ln2': jnp.ones((C,), jnp.float32), 'Wgate': w(ks[5], (C, E)), 'expert_bias': jnp.zeros((E,), jnp.float32), 'Wg': w(ks[6], (E, C, I)), 'Wu': w(ks[7], (E, C, I)), 'Wd': w(ks[8], (E, I, C)), 'sWg': w(ks[9], (S, C, I)), 'sWu': w(ks[10], (S, C, I)), 'sWd': w(ks[11], (S, I, C))}
    _L0_ffn_in = _L0_ffn_setup()
    _L0_c = _w((lambda *s: np.random.randn(*s).astype(np.float32) * 0.05)(4, 128))
    _L0_wmod = _w((lambda *s: np.random.randn(*s).astype(np.float32) * 0.05)(128, 6 * 128) * 128 ** (-0.5))

    def _L1_attn_setup():
        import jax, jax.numpy as jnp
        import numpy as np
        NUM_HEAD = 16
        D_Q = 64
        D_KV = 64
        ROPE_BASE = 10000.0

        def _cos_sin(seq_len, dim):
            pos = jnp.arange(seq_len, dtype=jnp.float32)[:, None]
            ids = jnp.arange(dim // 2, dtype=jnp.float32)
            theta = ROPE_BASE ** (-2.0 * ids) / (dim // 2)
            r = pos * theta[None, :]
            return (jnp.cos(r), jnp.sin(r))

        def _rope(x, cos, sin):
            b, s, d = x.shape
            xv = x.reshape(b, s, d // 2, 2)
            x0, x1 = (xv[..., 0], xv[..., 1])
            out = jnp.stack([x0 * cos - x1 * sin, x1 * cos + x0 * sin], axis=-1)
            return out.reshape(b, s, d)
        key = jax.random.key(seed)
        ks = jax.random.split(key, 10)
        d_model, d_q, d_kv = (128, D_Q, D_KV)
        b, s = (2, 256)
        w = lambda k, i, o: jax.random.normal(k, (i, o), dtype=jnp.float32) * 0.02
        return {'x': jax.random.normal(ks[0], (b, s, d_model), dtype=jnp.float32), 'Wd_q_w': w(ks[1], d_model, d_q), 'Wd_q_b': jnp.zeros((d_q,), jnp.float32), 'Wu_q_w': w(ks[2], d_q, d_model), 'Wu_q_b': jnp.zeros((d_model,), jnp.float32), 'Wq_r_w': w(ks[3], d_q, d_model), 'Wq_r_b': jnp.zeros((d_model,), jnp.float32), 'Wk_r_w': w(ks[4], d_model, d_model), 'Wk_r_b': jnp.zeros((d_model,), jnp.float32), 'Wd_kv_w': w(ks[5], d_model, d_kv), 'Wd_kv_b': jnp.zeros((d_kv,), jnp.float32), 'Wu_k_w': w(ks[6], d_kv, d_model), 'Wu_k_b': jnp.zeros((d_model,), jnp.float32), 'Wu_v_w': w(ks[7], d_kv, d_model), 'Wu_v_b': jnp.zeros((d_model,), jnp.float32), 'Wo_w': w(ks[8], d_model, d_model), 'Wo_b': jnp.zeros((d_model,), jnp.float32)}
    _L1_attn_in = _L1_attn_setup()

    def _L1_ffn_setup():
        import jax, jax.numpy as jnp
        import numpy as np
        B, S = (4, 256)
        D_MODEL, D_FF, N_EXPERTS, TOP_K = (128, 512, 8, 2)
        T = B * S
        CAPACITY_FACTOR, MIN_CAP = (1.25, 4)
        CAP = max(int(CAPACITY_FACTOR * (T * TOP_K / N_EXPERTS)), MIN_CAP)
        key = jax.random.key(seed)
        ks = jax.random.split(key, 6)

        def w(k, shape, fan):
            return jax.random.normal(k, shape, jnp.float32) * fan ** (-0.5)
        return {'x': jax.random.normal(ks[0], (B, S, D_MODEL), jnp.float32), 'Wr': w(ks[1], (D_MODEL, N_EXPERTS), D_MODEL), 'W1': w(ks[2], (N_EXPERTS, D_MODEL, D_FF), D_MODEL), 'b1': jnp.zeros((N_EXPERTS, D_FF), jnp.float32), 'W2': w(ks[3], (N_EXPERTS, D_FF, D_MODEL), D_FF), 'b2': jnp.zeros((N_EXPERTS, D_MODEL), jnp.float32), 'fw1': w(ks[4], (D_MODEL, D_FF), D_MODEL), 'fb1': jnp.zeros((D_FF,), jnp.float32), 'fw2': w(ks[5], (D_FF, D_MODEL), D_FF), 'fb2': jnp.zeros((D_MODEL,), jnp.float32)}
    _L1_ffn_in = _L1_ffn_setup()
    _L1_c = _w((lambda *s: np.random.randn(*s).astype(np.float32) * 0.05)(4, 128))
    _L1_wmod = _w((lambda *s: np.random.randn(*s).astype(np.float32) * 0.05)(128, 6 * 128) * 128 ** (-0.5))
    _d = {'L0_attn_x': _L0_attn_in['x'], 'L0_attn_W_in': _L0_attn_in['W_in'], 'L0_attn_b_in': _L0_attn_in['b_in'], 'L0_attn_conv_w': _L0_attn_in['conv_w'], 'L0_attn_conv_b': _L0_attn_in['conv_b'], 'L0_attn_A': _L0_attn_in['A'], 'L0_attn_C': _L0_attn_in['C'], 'L0_attn_Dp': _L0_attn_in['Dp'], 'L0_attn_W_out': _L0_attn_in['W_out'], 'L0_attn_b_out': _L0_attn_in['b_out'], 'L0_ffn_w_ln1': _L0_ffn_in['w_ln1'], 'L0_ffn_Wq': _L0_ffn_in['Wq'], 'L0_ffn_Wkva': _L0_ffn_in['Wkva'], 'L0_ffn_Wkvb': _L0_ffn_in['Wkvb'], 'L0_ffn_Wo': _L0_ffn_in['Wo'], 'L0_ffn_w_ln2': _L0_ffn_in['w_ln2'], 'L0_ffn_Wgate': _L0_ffn_in['Wgate'], 'L0_ffn_expert_bias': _L0_ffn_in['expert_bias'], 'L0_ffn_Wg': _L0_ffn_in['Wg'], 'L0_ffn_Wu': _L0_ffn_in['Wu'], 'L0_ffn_Wd': _L0_ffn_in['Wd'], 'L0_ffn_sWg': _L0_ffn_in['sWg'], 'L0_ffn_sWu': _L0_ffn_in['sWu'], 'L0_ffn_sWd': _L0_ffn_in['sWd'], 'L0_c': _L0_c, 'L0_wmod': _L0_wmod, 'L1_attn_Wd_q_w': _L1_attn_in['Wd_q_w'], 'L1_attn_Wd_q_b': _L1_attn_in['Wd_q_b'], 'L1_attn_Wu_q_w': _L1_attn_in['Wu_q_w'], 'L1_attn_Wu_q_b': _L1_attn_in['Wu_q_b'], 'L1_attn_Wq_r_w': _L1_attn_in['Wq_r_w'], 'L1_attn_Wq_r_b': _L1_attn_in['Wq_r_b'], 'L1_attn_Wk_r_w': _L1_attn_in['Wk_r_w'], 'L1_attn_Wk_r_b': _L1_attn_in['Wk_r_b'], 'L1_attn_Wd_kv_w': _L1_attn_in['Wd_kv_w'], 'L1_attn_Wd_kv_b': _L1_attn_in['Wd_kv_b'], 'L1_attn_Wu_k_w': _L1_attn_in['Wu_k_w'], 'L1_attn_Wu_k_b': _L1_attn_in['Wu_k_b'], 'L1_attn_Wu_v_w': _L1_attn_in['Wu_v_w'], 'L1_attn_Wu_v_b': _L1_attn_in['Wu_v_b'], 'L1_attn_Wo_w': _L1_attn_in['Wo_w'], 'L1_attn_Wo_b': _L1_attn_in['Wo_b'], 'L1_ffn_Wr': _L1_ffn_in['Wr'], 'L1_ffn_W1': _L1_ffn_in['W1'], 'L1_ffn_b1': _L1_ffn_in['b1'], 'L1_ffn_W2': _L1_ffn_in['W2'], 'L1_ffn_b2': _L1_ffn_in['b2'], 'L1_ffn_fw1': _L1_ffn_in['fw1'], 'L1_ffn_fb1': _L1_ffn_in['fb1'], 'L1_ffn_fw2': _L1_ffn_in['fw2'], 'L1_ffn_fb2': _L1_ffn_in['fb2'], 'L1_c': _L1_c, 'L1_wmod': _L1_wmod}
    _x0 = _d['L0_attn_x']
    _d['L0_attn_x'] = jax.random.normal(jax.random.fold_in(jax.random.key(seed), 1), (4, 1024, 128), dtype=_x0.dtype)
    del _x0
    return _d

def reference(L0_attn_x, L0_attn_W_in, L0_attn_b_in, L0_attn_conv_w, L0_attn_conv_b, L0_attn_A, L0_attn_C, L0_attn_Dp, L0_attn_W_out, L0_attn_b_out, L0_ffn_w_ln1, L0_ffn_Wq, L0_ffn_Wkva, L0_ffn_Wkvb, L0_ffn_Wo, L0_ffn_w_ln2, L0_ffn_Wgate, L0_ffn_expert_bias, L0_ffn_Wg, L0_ffn_Wu, L0_ffn_Wd, L0_ffn_sWg, L0_ffn_sWu, L0_ffn_sWd, L0_c, L0_wmod, L1_attn_Wd_q_w, L1_attn_Wd_q_b, L1_attn_Wu_q_w, L1_attn_Wu_q_b, L1_attn_Wq_r_w, L1_attn_Wq_r_b, L1_attn_Wk_r_w, L1_attn_Wk_r_b, L1_attn_Wd_kv_w, L1_attn_Wd_kv_b, L1_attn_Wu_k_w, L1_attn_Wu_k_b, L1_attn_Wu_v_w, L1_attn_Wu_v_b, L1_attn_Wo_w, L1_attn_Wo_b, L1_ffn_Wr, L1_ffn_W1, L1_ffn_b1, L1_ffn_W2, L1_ffn_b2, L1_ffn_fw1, L1_ffn_fb1, L1_ffn_fw2, L1_ffn_fb2, L1_c, L1_wmod):

    def _L0_attn_ref(x, W_in, b_in, conv_w, conv_b, A, C, Dp, W_out, b_out):
        import jax, jax.numpy as jnp
        import numpy as np
        D_MODEL = 128
        D_STATE = 16
        D_CONV = 4
        EXPAND = 2
        E = EXPAND * D_MODEL
        B, L = (4, 512)
        Bb, Ll, _ = x.shape
        x_and_z = x @ W_in + b_in
        x_proj, z = jnp.split(x_and_z, 2, axis=-1)
        xc = jnp.transpose(x_proj, (0, 2, 1))
        xc = jax.lax.conv_general_dilated(xc, conv_w, window_strides=(1,), padding=[(D_CONV - 1, 0)], dimension_numbers=('NCH', 'OIH', 'NCH'), feature_group_count=E)
        x_conv = jnp.transpose(xc + conv_b[None, :, None], (0, 2, 1))

        def step(h, xt):
            h = jnp.tanh(xt @ A + h)
            yt = h @ C.T + Dp * xt
            return (h, yt)
        h0 = jnp.zeros((Bb, D_STATE), dtype=x.dtype)
        _, ys = jax.lax.scan(step, h0, jnp.transpose(x_conv, (1, 0, 2)))
        x_s4 = jnp.transpose(ys, (1, 0, 2))
        y = jax.nn.sigmoid(z) * x_s4
        return y @ W_out + b_out

    def _L0_ffn_ref(x, w_ln1, Wq, Wkva, Wkvb, Wo, w_ln2, Wgate, expert_bias, Wg, Wu, Wd, sWg, sWu, sWd):
        import jax, jax.numpy as jnp
        import numpy as np
        B, T, C = (2, 256, 128)
        H, D = (16, 64)
        CR = 8
        R = C // CR
        ROPE = D // 2
        NOPE = D - ROPE
        E, K, I, S = (8, 2, 64, 1)
        THETA = 100000.0
        EPS = 1e-05

        def _rmsnorm(x, w):
            rms = jnp.sqrt(jnp.mean(x * x, axis=-1, keepdims=True) + EPS)
            return w * (x / rms)

        def _rope(xh):
            d = xh.shape[-1]
            t = jnp.arange(xh.shape[2], dtype=jnp.float32)
            freqs = 1.0 / THETA ** (jnp.arange(0, d, 2, dtype=jnp.float32) / d)
            ang = jnp.outer(t, freqs)
            cos, sin = (jnp.cos(ang), jnp.sin(ang))
            xr = xh.reshape(xh.shape[:-1] + (d // 2, 2))
            x0, x1 = (xr[..., 0], xr[..., 1])
            rot = jnp.stack([x0 * cos - x1 * sin, x0 * sin + x1 * cos], axis=-1)
            return rot.reshape(xh.shape)

        def _attention(x, Wq, Wkva, Wkvb, Wo):
            b, t, _ = x.shape
            q = (x @ Wq).reshape(b, t, H, D).transpose(0, 2, 1, 3)
            ckv = x @ Wkva
            kv_latent, k_rope = (ckv[:, :, :R], ckv[:, :, R:])
            kv = (kv_latent @ Wkvb).reshape(b, t, H, NOPE).transpose(0, 2, 1, 3)
            k_rope = jnp.broadcast_to(k_rope[:, None, :, :], (b, H, t, ROPE))
            q_nope, q_rope = (q[..., :NOPE], q[..., NOPE:])
            q = jnp.concatenate([q_nope, _rope(q_rope)], axis=-1)
            k = jnp.concatenate([kv, _rope(k_rope)], axis=-1)
            v = jnp.concatenate([kv, jnp.zeros_like(k_rope)], axis=-1)
            att = jnp.einsum('bhqd,bhkd->bhqk', q, k) / jnp.sqrt(jnp.float32(D))
            mask = jnp.tril(jnp.ones((t, t), dtype=bool))
            att = jnp.where(mask, att, jnp.float32(-jnp.inf))
            att = jax.nn.softmax(att, axis=-1)
            y = jnp.einsum('bhqk,bhkd->bhqd', att, v)
            y = y.transpose(0, 2, 1, 3).reshape(b, t, H * D)
            return y @ Wo

        def _experts(x_flat, Wg, Wu, Wd):
            g = jax.nn.silu(jnp.einsum('nc,eci->nei', x_flat, Wg))
            u = jnp.einsum('nc,eci->nei', x_flat, Wu)
            return jnp.einsum('nei,eic->nec', g * u, Wd)

        def _moe(x, Wgate, expert_bias, Wg, Wu, Wd, sWg, sWu, sWd):
            b, t, c = x.shape
            xf = x.reshape(-1, c)
            shared = jnp.mean(_experts(xf, sWg, sWu, sWd), axis=1)
            logits = xf @ Wgate + expert_bias
            probs = jax.nn.softmax(logits, axis=-1)
            topk_p, topk_i = jax.lax.top_k(probs, K)
            topk_p = topk_p / jnp.sum(topk_p, axis=-1, keepdims=True)
            comb = jnp.sum(jax.nn.one_hot(topk_i, E, dtype=xf.dtype) * topk_p[..., None], axis=1)
            routed = jnp.einsum('ne,nec->nc', comb, _experts(xf, Wg, Wu, Wd))
            return (shared + routed).reshape(b, t, c)
        x = x + _attention(_rmsnorm(x, w_ln1), Wq, Wkva, Wkvb, Wo)
        residual = x
        xn = _rmsnorm(x, w_ln2)
        x_out = _moe(xn, Wgate, expert_bias, Wg, Wu, Wd, sWg, sWu, sWd)
        return residual + x_out

    def _L1_attn_ref(x, Wd_q_w, Wd_q_b, Wu_q_w, Wu_q_b, Wq_r_w, Wq_r_b, Wk_r_w, Wk_r_b, Wd_kv_w, Wd_kv_b, Wu_k_w, Wu_k_b, Wu_v_w, Wu_v_b, Wo_w, Wo_b):
        import jax, jax.numpy as jnp
        import numpy as np
        NUM_HEAD = 16
        D_Q = 64
        D_KV = 64
        ROPE_BASE = 10000.0

        def _cos_sin(seq_len, dim):
            pos = jnp.arange(seq_len, dtype=jnp.float32)[:, None]
            ids = jnp.arange(dim // 2, dtype=jnp.float32)
            theta = ROPE_BASE ** (-2.0 * ids) / (dim // 2)
            r = pos * theta[None, :]
            return (jnp.cos(r), jnp.sin(r))

        def _rope(x, cos, sin):
            b, s, d = x.shape
            xv = x.reshape(b, s, d // 2, 2)
            x0, x1 = (xv[..., 0], xv[..., 1])
            out = jnp.stack([x0 * cos - x1 * sin, x1 * cos + x0 * sin], axis=-1)
            return out.reshape(b, s, d)
        b, s, d_model = x.shape
        h = NUM_HEAD
        hd = d_model // h
        scale = jnp.sqrt(jnp.float32(h + D_KV + D_Q))

        def heads(t):
            return t.reshape(b, s, h, hd).transpose(0, 2, 1, 3)
        cos, sin = _cos_sin(s, d_model)
        ct_q = x @ Wd_q_w + Wd_q_b
        qt_c = heads(ct_q @ Wu_q_w + Wu_q_b)
        qt_r = heads(_rope(ct_q @ Wq_r_w + Wq_r_b, cos, sin))
        query = qt_c + qt_r
        ct_kv = x @ Wd_kv_w + Wd_kv_b
        kt_c = heads(ct_kv @ Wu_k_w + Wu_k_b)
        kt_r = heads(_rope(x @ Wk_r_w + Wk_r_b, cos, sin))
        key = kt_c + kt_r
        value = heads(ct_kv @ Wu_v_w + Wu_v_b)
        attn = jnp.einsum('bhqd,bhkd->bhqk', query, key) / scale
        attn = jax.nn.softmax(attn, axis=-1)
        out = jnp.einsum('bhqk,bhkd->bhqd', attn, value)
        out = out.transpose(0, 2, 1, 3).reshape(b, s, d_model)
        return out @ Wo_w + Wo_b

    def _L1_ffn_ref(x, Wr, W1, b1, W2, b2, fw1, fb1, fw2, fb2):
        import jax, jax.numpy as jnp
        import numpy as np
        B, S = (4, 256)
        D_MODEL, D_FF, N_EXPERTS, TOP_K = (128, 512, 8, 2)
        T = B * S
        CAPACITY_FACTOR, MIN_CAP = (1.25, 4)
        CAP = max(int(CAPACITY_FACTOR * (T * TOP_K / N_EXPERTS)), MIN_CAP)
        Bx, Sx, D = x.shape
        Tn = Bx * Sx
        xf = x.reshape(Tn, D)
        logits = xf @ Wr
        probs = jax.nn.softmax(logits, axis=-1)
        scores, experts = jax.lax.top_k(probs, TOP_K)
        scores = scores / jnp.maximum(scores.sum(-1, keepdims=True), 1e-09)
        y_fb = jax.nn.gelu(xf @ fw1 + fb1, approximate=False) @ fw2 + fb2
        y = jnp.zeros_like(xf)
        fb_mask = jnp.zeros((Tn,), bool)
        for e in range(N_EXPERTS):
            assign = experts == e
            w_e = jnp.where(assign, scores, 0.0).sum(-1)
            eligible = assign.any(-1) & ~fb_mask
            rank = jnp.cumsum(eligible.astype(jnp.int32)) - 1
            keep = eligible & (rank < CAP)
            overflow = eligible & ~keep
            fb_mask = fb_mask | overflow
            y = jnp.where(overflow[:, None], y_fb, y)
            idx = jnp.nonzero(keep, size=CAP, fill_value=0)[0]
            valid = jnp.arange(CAP) < keep.sum()
            h = jax.nn.gelu(xf[idx] @ W1[e] + b1[e], approximate=False)
            y_e = h @ W2[e] + b2[e]
            y = y.at[idx].add(y_e * (w_e[idx] * valid)[:, None])
        return y.reshape(Bx, Sx, D)
    x = L0_attn_x
    mod = (_silu(L0_c) @ L0_wmod).reshape(L0_c.shape[0], 6, 1, -1)
    sa, ca, ga, sb, cb, gb = (mod[:, 0], mod[:, 1], mod[:, 2], mod[:, 3], mod[:, 4], mod[:, 5])
    ga = (2 * (ga >= 0) - 1) * jnp.maximum(jnp.abs(ga), 0.25)
    gb = (2 * (gb >= 0) - 1) * jnp.maximum(jnp.abs(gb), 0.25)
    h = _layernorm(x, axis=-1) * (1 + ca) + sa
    x = x + ga * _L0_attn_ref(h, L0_attn_W_in, L0_attn_b_in, L0_attn_conv_w, L0_attn_conv_b, L0_attn_A, L0_attn_C, L0_attn_Dp, L0_attn_W_out, L0_attn_b_out)
    h = _layernorm(x, axis=-1) * (1 + cb) + sb
    x = x + gb * _L0_ffn_ref(h, L0_ffn_w_ln1, L0_ffn_Wq, L0_ffn_Wkva, L0_ffn_Wkvb, L0_ffn_Wo, L0_ffn_w_ln2, L0_ffn_Wgate, L0_ffn_expert_bias, L0_ffn_Wg, L0_ffn_Wu, L0_ffn_Wd, L0_ffn_sWg, L0_ffn_sWu, L0_ffn_sWd)
    mod = (_silu(L1_c) @ L1_wmod).reshape(L1_c.shape[0], 6, 1, -1)
    sa, ca, ga, sb, cb, gb = (mod[:, 0], mod[:, 1], mod[:, 2], mod[:, 3], mod[:, 4], mod[:, 5])
    ga = (2 * (ga >= 0) - 1) * jnp.maximum(jnp.abs(ga), 0.25)
    gb = (2 * (gb >= 0) - 1) * jnp.maximum(jnp.abs(gb), 0.25)
    h = _layernorm(x, axis=-1) * (1 + ca) + sa
    x = x + ga * _L1_attn_ref(h, L1_attn_Wd_q_w, L1_attn_Wd_q_b, L1_attn_Wu_q_w, L1_attn_Wu_q_b, L1_attn_Wq_r_w, L1_attn_Wq_r_b, L1_attn_Wk_r_w, L1_attn_Wk_r_b, L1_attn_Wd_kv_w, L1_attn_Wd_kv_b, L1_attn_Wu_k_w, L1_attn_Wu_k_b, L1_attn_Wu_v_w, L1_attn_Wu_v_b, L1_attn_Wo_w, L1_attn_Wo_b)
    h = _layernorm(x, axis=-1) * (1 + cb) + sb
    x = x + gb * _L1_ffn_ref(h, L1_ffn_Wr, L1_ffn_W1, L1_ffn_b1, L1_ffn_W2, L1_ffn_b2, L1_ffn_fw1, L1_ffn_fb1, L1_ffn_fw2, L1_ffn_fb2)
    return x

_drawn_inputs = setup_inputs


def setup_inputs(seed=0):
    import zlib

    import numpy as np

    out = dict(_drawn_inputs(seed))
    spreads = {'L0_attn_b_in': (0.0, 0.8),
     'L0_attn_conv_b': (0.0, 0.8),
     'L0_attn_Dp': (0.009999999776482582, 0.6),
     'L0_attn_b_out': (0.0, 0.269),
     'L0_ffn_w_ln1': (1.0, 0.6),
     'L0_ffn_w_ln2': (1.0, 0.6),
     'L0_ffn_expert_bias': (0.0, 0.8),
     'L1_attn_Wd_q_b': (0.0, 0.8),
     'L1_attn_Wu_q_b': (0.0, 2.0),
     'L1_attn_Wq_r_b': (0.0, 2.0),
     'L1_attn_Wk_r_b': (0.0, 2.0),
     'L1_attn_Wd_kv_b': (0.0, 0.8),
     'L1_attn_Wu_k_b': (0.0, 2.0),
     'L1_attn_Wu_v_b': (0.0, 0.735),
     'L1_attn_Wo_b': (0.0, 0.736),
     'L1_ffn_b1': (0.0, 2.0),
     'L1_ffn_b2': (0.0, 2.0),
     'L1_ffn_fb1': (0.0, 1.774),
     'L1_ffn_fb2': (0.0, 1.19)}
    factors = {'L0_attn_W_in': 8.0,
     'L0_attn_conv_w': 8.0,
     'L0_attn_A': 8.0,
     'L0_attn_C': 8.0,
     'L0_attn_W_out': 8.0,
     'L0_ffn_Wq': 8.0,
     'L0_ffn_Wkva': 8.0,
     'L0_ffn_Wkvb': 8.0,
     'L0_ffn_Wo': 8.0,
     'L0_ffn_Wgate': 8.0,
     'L0_ffn_Wg': 8.0,
     'L0_ffn_Wu': 8.0,
     'L0_ffn_Wd': 8.0,
     'L0_ffn_sWg': 8.0,
     'L0_ffn_sWu': 8.0,
     'L0_ffn_sWd': 8.0,
     'L1_attn_Wd_q_w': 8.0,
     'L1_attn_Wu_q_w': 8.0,
     'L1_attn_Wq_r_w': 8.0,
     'L1_attn_Wk_r_w': 8.0,
     'L1_attn_Wd_kv_w': 8.0,
     'L1_attn_Wu_k_w': 8.0,
     'L1_attn_Wu_v_w': 8.0,
     'L1_attn_Wo_w': 5.405,
     'L1_ffn_W1': 2.848}
    for name, (base, spread) in spreads.items():
        noise = np.random.default_rng([zlib.crc32(name.encode()), seed]).standard_normal(out[name].shape)
        drawn = base * np.exp(spread * noise) if base else spread * noise
        out[name] = jnp.asarray(drawn.astype(out[name].dtype))
    for name, factor in factors.items():
        out[name] = (out[name] * factor).astype(out[name].dtype)
    return out
```

```python
import numpy as np
from contextlib import ExitStack, contextmanager

import concourse.bass as bass
from concourse import mybir

F32 = mybir.dt.float32
BF16 = mybir.dt.bfloat16
ALU = mybir.AluOpType
ACT = mybir.ActivationFunctionType
AX = mybir.AxisListType

B, T, D = 4, 1024, 128
N = B * T
E = 256
NS = 16
H = 16
HG = 4
NG = H // HG
CH = 512
LN_EPS = 1e-5
NEG = -1e30

VEC = {}
for _name, _n in (("b_in", 4), ("conv_w", 8), ("conv_b", 2), ("Dp", 2), ("b_out", 1), ("ln1", 1), ("ln2", 1),
                  ("Wu_q_b", 1), ("Wq_r_b", 1), ("Wq_r_bs", 1), ("Wk_r_b", 1), ("Wk_r_bs", 1), ("Wu_k_b", 1),
                  ("Wo_b", 1), ("b1", 32), ("b2", 8), ("fb1", 4), ("fb2", 1)):
    VEC[_name] = (sum(n for _, n in VEC.values()), _n)
NVEC = sum(n for _, n in VEC.values())


class State:

    def vec(self, name, k=0):
        return self.vecs[:, VEC[name][0] + k:VEC[name][0] + k + 1]


def batch(b, c=None):
    return slice(b * T, (b + 1) * T) if c is None else slice(b * T + c * CH, b * T + (c + 1) * CH)


@contextmanager
def stage(nc):
    with ExitStack() as ctx:
        ctx.sems = []
        yield ctx
    if ctx.sems:
        with nc.Block() as block:
            @block.gpsimd
            def _(pool):
                nc.clear_and_free_semaphores(ctx.sems)


def semaphore(nc, ctx, name):
    ctx.sems.append(nc.alloc_semaphore(name))
    return ctx.sems[-1]


def setup(nc, S, A):
    with stage(nc) as ctx:
        cT = ctx.enter_context(nc.sbuf_tensor("cT", [D, 2, B], F32))
        cs = ctx.enter_context(nc.sbuf_tensor("cs", [D, 2, B], F32))
        wm = ctx.enter_context(nc.sbuf_tensor("wm", [D, 2, 6 * D], F32))
        sign = ctx.enter_context(nc.sbuf_tensor("sign", [D, B], F32))
        mag = ctx.enter_context(nc.sbuf_tensor("mag", [D, B], F32))
        ps = ctx.enter_context(nc.psum_tensor("ps_mod", [D, 2, 6, B], F32))
        loaded = semaphore(nc, ctx, "loaded")
        silu_done = semaphore(nc, ctx, "silu_done")
        mod_ready = semaphore(nc, ctx, "mod_ready")
        chain = semaphore(nc, ctx, "setup_chain")
        block = ctx.enter_context(nc.Block())

        @block.sync
        def _(sp):
            sp.dma_start(cT[:, 0, :], A["c0T"]).then_inc(loaded, 16)
            sp.dma_start(cT[:, 1, :], A["c1T"]).then_inc(loaded, 16)
            sp.dma_start(wm[:, 0, :], A["wmod0"]).then_inc(loaded, 16)
            sp.dma_start(wm[:, 1, :], A["wmod1"]).then_inc(loaded, 16)
            sp.dma_start(S.vecs[:, :], A["vecs"]).then_inc(loaded, 16)
            sp.dma_start(S.ident[:, :], A["ident"]).then_inc(loaded, 16)
            sp.dma_start(S.mean_sel[:, :, :], A["mean_sel"].rearrange("p (j q) -> p j q", q=D)).then_inc(loaded, 16)
            sp.dma_start(S.spread[:, :, :], A["spread"].rearrange("p (j q) -> p j q", q=D)).then_inc(loaded, 16)
            for b in range(B):
                sp.dma_start(S.xT[:, batch(b)], A["xT"][:, batch(b)]).then_inc(loaded, 16)
            sp.wait_ge(loaded, 192)

        @block.scalar
        def _(act):
            act.wait_ge(loaded, 192)
            act.activation(cs[:, :, :], cT[:, :, :], ACT.Silu).then_inc(silu_done, 1)

        @block.tensor
        def _(pe):
            pe.wait_ge(silu_done, 1)
            for l in range(2):
                for j in range(6):
                    last = pe.matmul(ps[:, l, j, :], wm[:, l, j * D:(j + 1) * D], cs[:, l, :], start=True, stop=True)
            last.then_inc(mod_ready, 1)

        @block.vector
        def _(dve):
            n = 0

            def link(ins):
                nonlocal n
                n += 1
                ins.then_inc(chain, 1)
                dve.wait_ge(chain, n)

            dve.memset(S.mean[:, :], 1.0 / D)
            dve.wait_ge(loaded, 192)
            dve.tensor_copy(S.ident_bf[:, :], S.ident[:, :])
            dve.wait_ge(mod_ready, 1)
            link(dve.tensor_copy(S.mod[:, :, :, :], ps[:, :, :, :]))
            for l in range(2):
                for j in (1, 4):
                    link(dve.tensor_scalar_add(S.mod[:, l, j, :], S.mod[:, l, j, :], 1.0))
                for j in (2, 5):
                    g = S.mod[:, l, j, :]
                    link(dve.tensor_scalar(sign[:, :], g, 0.0, 2.0, ALU.is_ge, ALU.mult))
                    link(dve.tensor_scalar_add(sign[:, :], sign[:, :], -1.0))
                    link(dve.scalar_tensor_tensor(out=mag[:, :], in0=g, scalar=-1.0, in1=g, op0=ALU.mult, op1=ALU.max))
                    link(dve.tensor_scalar_max(mag[:, :], mag[:, :], 0.25))
                    link(dve.tensor_tensor(g, mag[:, :], sign[:, :], ALU.mult))


def layernorm(nc, S, l, kind):
    shift, scale = 3 * kind, 3 * kind + 1
    with stage(nc) as ctx:
        xc = ctx.enter_context(nc.sbuf_tensor(f"xc{l}{kind}", [D, N], F32))
        sq = ctx.enter_context(nc.sbuf_tensor(f"sq{l}{kind}", [D, N], F32))
        rows = ctx.enter_context(nc.sbuf_tensor(f"rows{l}{kind}", [D, CH], F32))
        ps = ctx.enter_context(nc.psum_tensor(f"ps_ln{l}{kind}", [D, N], F32))
        sems = [semaphore(nc, ctx, f"ln{l}{kind}_{x}") for x in
                ("mean", "centered", "squared", "variance", "deviation", "inverted", "spread", "scaled", "shifted")]
        mean, centered, squared, variance, deviation, inverted, spread, scaled, shifted = sems
        block = ctx.enter_context(nc.Block())

        @block.tensor
        def _(pe):
            for b in range(B):
                for c in range(2):
                    last = pe.matmul(ps[:, batch(b, c)], S.mean[:, :], S.xT[:, batch(b, c)], start=True, stop=True)
                last.then_inc(mean, 1)
            for b in range(B):
                pe.wait_ge(squared, b + 1)
                for c in range(2):
                    j = 2 * b + c
                    last = pe.matmul(ps[:, 0:CH], S.mean_sel[:, j, :], sq[:, batch(b, c)], start=(j == 0), stop=(j == 2 * B - 1))
            last.then_inc(variance, 1)
            pe.wait_ge(inverted, 1)
            for b in range(B):
                for c in range(2):
                    last = pe.matmul(ps[:, batch(b, c)], S.spread[:, 2 * b + c, :], rows[:, :], start=True, stop=True)
                last.then_inc(spread, 1)

        @block.scalar
        def _(act):
            for b in range(B):
                act.wait_ge(centered, b + 1)
                act.activation(sq[:, batch(b)], xc[:, batch(b)], ACT.Square).then_inc(squared, 1)
            act.wait_ge(variance, 1)
            act.activation(rows[:, :], ps[:, 0:CH], ACT.Sqrt, bias=S.eps[:, 0:1]).then_inc(deviation, 1)
            for b in range(B):
                act.wait_ge(scaled, b + 1)
                act.activation(S.hT[:, batch(b)], S.hT[:, batch(b)], ACT.Identity,
                               bias=S.mod[:, l, shift, b:b + 1]).then_inc(shifted, 1)

        @block.vector
        def _(dve):
            for b in range(B):
                dve.wait_ge(mean, b + 1)
                dve.tensor_tensor(xc[:, batch(b)], S.xT[:, batch(b)], ps[:, batch(b)], ALU.subtract).then_inc(centered, 1)
            dve.wait_ge(deviation, 1)
            dve.reciprocal(rows[:, :], rows[:, :]).then_inc(inverted, 1)
            for b in range(B):
                dve.wait_ge(spread, b + 1)
                dve.scalar_tensor_tensor(out=S.hT[:, batch(b)], in0=xc[:, batch(b)], scalar=S.mod[:, l, scale, b:b + 1],
                                         in1=ps[:, batch(b)], op0=ALU.mult, op1=ALU.mult).then_inc(scaled, 1)


def rmsnorm(nc, S, src, dst, weight, name):
    with stage(nc) as ctx:
        sq = ctx.enter_context(nc.sbuf_tensor(f"sq_{name}", [D, N], F32))
        rows = ctx.enter_context(nc.sbuf_tensor(f"rows_{name}", [D, CH], F32))
        ps = ctx.enter_context(nc.psum_tensor(f"ps_{name}", [D, N], F32))
        squared, meansq, root, inverted, spread = [semaphore(nc, ctx, f"{name}_{x}") for x in
                                           ("squared", "meansq", "root", "inverted", "spread")]
        block = ctx.enter_context(nc.Block())

        @block.scalar
        def _(act):
            for b in range(B):
                act.activation(sq[:, batch(b)], src[:, batch(b)], ACT.Square).then_inc(squared, 1)
            act.wait_ge(meansq, 1)
            act.activation(rows[:, :], ps[:, 0:CH], ACT.Sqrt, bias=S.eps[:, 0:1]).then_inc(root, 1)

        @block.tensor
        def _(pe):
            for b in range(B):
                pe.wait_ge(squared, b + 1)
                for c in range(2):
                    j = 2 * b + c
                    last = pe.matmul(ps[:, 0:CH], S.mean_sel[:, j, :], sq[:, batch(b, c)], start=(j == 0), stop=(j == 2 * B - 1))
            last.then_inc(meansq, 1)
            pe.wait_ge(inverted, 1)
            for b in range(B):
                for c in range(2):
                    last = pe.matmul(ps[:, batch(b, c)], S.spread[:, 2 * b + c, :], rows[:, :], start=True, stop=True)
                last.then_inc(spread, 1)

        @block.vector
        def _(dve):
            dve.wait_ge(root, 1)
            dve.reciprocal(rows[:, :], rows[:, :]).then_inc(inverted, 1)
            for b in range(B):
                dve.wait_ge(spread, b + 1)
                dve.scalar_tensor_tensor(out=dst[:, batch(b)], in0=src[:, batch(b)], scalar=S.vec(weight),
                                         in1=ps[:, batch(b)], op0=ALU.mult, op1=ALU.mult)


def recurrent(nc, S, A):
    PAD = 3
    with ExitStack() as outer:
        xconv = outer.enter_context(nc.sbuf_tensor("xconv", [128, 2, N], F32))
        sz = outer.enter_context(nc.sbuf_tensor("sz", [128, 2, N], F32))
        A_sb = outer.enter_context(nc.sbuf_tensor("A_sb", [128, 2, 32], F32))
        CT_sb = outer.enter_context(nc.sbuf_tensor("CT_sb", [128, E], F32))
        Wout_sb = outer.enter_context(nc.sbuf_tensor("Wout_sb", [128, 2, D], F32))
        hs = outer.enter_context(nc.sbuf_tensor("hs", [128, 1 + T], F32))

        with stage(nc) as ctx:
            W_in = ctx.enter_context(nc.sbuf_tensor("W_in", [D, 4 * 128], F32))
            xp = ctx.enter_context(nc.sbuf_tensor("xp", [128, 2, B, PAD + T], F32))
            ps = ctx.enter_context(nc.psum_tensor("ps_in", [128, 2, 2, T], F32))
            loaded = semaphore(nc, ctx, "ssm_loaded")
            in_loaded = semaphore(nc, ctx, "ssm_in_loaded")
            padded = semaphore(nc, ctx, "ssm_padded")
            projected = semaphore(nc, ctx, "ssm_projected")
            evacuated = semaphore(nc, ctx, "ssm_evacuated")
            tapped = semaphore(nc, ctx, "ssm_tapped")
            block = ctx.enter_context(nc.Block())

            @block.sync
            def _(sp):
                sp.dma_start(W_in[:, :], A["W_in"]).then_inc(in_loaded, 16)
                sp.wait_ge(padded, 1)
                sp.dma_start(A_sb[:, :, 0:NS], A["A"].rearrange("(m p) n -> p m n", p=128)).then_inc(loaded, 16)
                for b in range(B):
                    sp.dma_start(CT_sb[32 * b:32 * b + NS, :], A["CT"]).then_inc(loaded, 16)
                sp.dma_start(Wout_sb[:, :, :], A["W_out"].rearrange("(m p) n -> p m n", p=128)).then_inc(loaded, 16)
                sp.wait_ge(loaded, 16 * 6)

            @block.gpsimd
            def _(pool):
                pool.memset(A_sb[:, :, :], 0.0)
                pool.memset(xp[:, :, :, 0:PAD], 0.0)
                pool.memset(CT_sb[:, :], 0.0)
                pool.drain().then_inc(padded, 1)

            @block.tensor
            def _(pe):
                pe.wait_ge(in_loaded, 16)
                for r in range(2 * B):
                    b, kind = r // 2, r % 2
                    if r >= 2:
                        pe.wait_ge(evacuated, 2 * (r - 1))
                    for m in range(2):
                        w = W_in[:, (2 * kind + m) * 128:(2 * kind + m + 1) * 128]
                        for c in range(2):
                            last = pe.matmul(ps[:, r % 2, m, c * CH:(c + 1) * CH], w, S.hT[:, batch(b, c)],
                                             start=True, stop=True)
                    last.then_inc(projected, 1)

            @block.scalar
            def _(act):
                act.wait_ge(padded, 1)
                for r in range(2 * B):
                    b, kind = r // 2, r % 2
                    act.wait_ge(projected, r + 1)
                    for m in range(2):
                        to = sz[:, m, batch(b)] if kind else xp[:, m, b, PAD:PAD + T]
                        act.activation(to, ps[:, r % 2, m, :], ACT.Sigmoid if kind else ACT.Identity,
                                       bias=S.vec("b_in", 2 * kind + m)).then_inc(evacuated, 1)

            @block.vector
            def _(dve):
                n = 0
                for b in range(B):
                    dve.wait_ge(evacuated, 4 * b + 2)
                    for k in range(PAD, -1, -1):
                        for m in range(2):
                            x, w, acc = xp[:, m, b, k:k + T], S.vec("conv_w", 4 * m + k), xconv[:, m, batch(b)]
                            if k == PAD:
                                ins = dve.tensor_scalar(acc, x, w, S.vec("conv_b", m), ALU.mult, ALU.add)
                            else:
                                dve.wait_ge(tapped, n - 1)
                                ins = dve.scalar_tensor_tensor(out=acc, in0=x, scalar=w, in1=acc, op0=ALU.mult, op1=ALU.add)
                            ins.then_inc(tapped, 1)
                            n += 1

        with stage(nc) as ctx:
            ROUNDS, TOLERANCE, STEPS = 8, 1e-5, 64
            f, r, slope, d = [ctx.enter_context(nc.sbuf_tensor("newton_" + x, [128, T], F32)) for x in ("f", "r", "slope", "d")]
            worst = ctx.enter_context(nc.sbuf_tensor("worst", [128, 2], F32))
            failed = ctx.enter_context(nc.sbuf_tensor("failed", [1, 1], mybir.dt.int32))
            u = ctx.enter_context(nc.psum_tensor("u", [128, T], F32))
            worst_row = ctx.enter_context(nc.psum_tensor("worst_row", [1, 128], F32))
            driven, stepped = semaphore(nc, ctx, "ssm_driven"), semaphore(nc, ctx, "ssm_stepped")
            added, tanh_done, squared, residual, sloped, scanned, corrected = [
                semaphore(nc, ctx, "newton_" + x) for x in ("added", "tanh", "squared", "residual", "sloped", "scanned", "corrected")]
            judged, worst_turned = semaphore(nc, ctx, "newton_judged"), semaphore(nc, ctx, "newton_turned")
            block = ctx.enter_context(nc.Block())

            @block.tensor
            def _(pe):
                for c in range(2):
                    for b in range(B):
                        for m in range(2):
                            last = pe.matmul(u[32 * b:32 * b + 32, c * CH:(c + 1) * CH], A_sb[:, m, :],
                                             xconv[:, m, batch(b, c)], start=(m == 0), stop=(m == 1))
                last.then_inc(driven, 1)
                pe.wait_ge(judged, 2)
                pe.transpose(worst_row[:, :], worst[:, 0:1], S.ident[:, :]).then_inc(worst_turned, 1)

            @block.vector
            def _(dve):
                dve.memset(hs[:, :], 0.0).then_inc(corrected, 1)
                dve.wait_ge(driven, 1)
                with dve.Fori(0, ROUNDS) as i:
                    dve.wait_ge(corrected, i + 1)
                    dve.tensor_tensor(f[:, :], u[:, :], hs[:, 0:T], ALU.add).then_inc(added, 1)
                    dve.wait_ge(tanh_done, i + 1)
                    dve.tensor_tensor(r[:, :], f[:, :], hs[:, 1:1 + T], ALU.subtract).then_inc(residual, 1)
                    dve.wait_ge(squared, i + 1)
                    dve.tensor_scalar(slope[:, :], slope[:, :], -1.0, 1.0, ALU.mult, ALU.add).then_inc(sloped, 1)
                    dve.wait_ge(residual, i + 1)
                    dve.wait_ge(sloped, i + 1)
                    dve.tensor_tensor_scan(d[:, :], slope[:, :], r[:, :], 0.0, ALU.mult, ALU.add).then_inc(scanned, 1)
                    dve.wait_ge(scanned, i + 1)
                    dve.tensor_tensor(hs[:, 1:1 + T], hs[:, 1:1 + T], d[:, :], ALU.add).then_inc(corrected, 1)
                dve.wait_ge(corrected, ROUNDS + 1)
                dve.tensor_tensor(d[:, :], r[:, :], r[:, :], ALU.mult).then_inc(judged, 1)
                dve.wait_ge(judged, 1)
                dve.tensor_reduce(worst[:, 0:1], d[:, :], AX.X, ALU.max).then_inc(judged, 1)
                dve.wait_ge(worst_turned, 1)
                dve.tensor_reduce(worst[0:1, 1:2], worst_row[:, :], AX.X, ALU.max).then_inc(judged, 1)
                dve.wait_ge(judged, 3)
                dve.tensor_scalar(failed[:, :], worst[0:1, 1:2], TOLERANCE ** 2, None, ALU.is_gt).then_inc(judged, 1)

            @block.scalar
            def _(act):
                with act.Fori(0, ROUNDS) as i:
                    act.wait_ge(added, i + 1)
                    act.activation(f[:, :], f[:, :], ACT.Tanh).then_inc(tanh_done, 1)
                    act.wait_ge(tanh_done, i + 1)
                    act.activation(slope[:, :], f[:, :], ACT.Square).then_inc(squared, 1)
                act.wait_ge(judged, 4)
                act.wait_ge(corrected, ROUNDS + 1)
                with act.If(act.value_load(failed[0:1, 0:1], min_val=0, max_val=1) > 0):
                    act.sem_inc(stepped, 1)
                    with act.Fori(0, T // STEPS) as i:
                        for j in range(STEPS):
                            act.wait_ge(stepped, i * STEPS + (j + 1))
                            act.activation(hs[:, bass.ds(i * STEPS + (j + 1), 1)], u[:, bass.ds(i * STEPS + j, 1)], ACT.Tanh,
                                           bias=hs[:, bass.ds(i * STEPS + j, 1)]).then_inc(stepped, 1)
                act.drain()

        with stage(nc) as ctx:
            ps_y = ctx.enter_context(nc.psum_tensor("ps_y", [128, 2, T], F32))
            ps_o = ctx.enter_context(nc.psum_tensor("ps_o", [128, 2, T], F32))
            o = ctx.enter_context(nc.sbuf_tensor("o_ssm", [128, 2, T], F32))
            read, skipped, gated, out_ready, biased, added = [
                semaphore(nc, ctx, f"ssm_{x}") for x in ("read", "skipped", "gated", "out", "biased", "added")]
            block = ctx.enter_context(nc.Block())

            @block.tensor
            def _(pe):
                for b in range(B + 1):
                    if b < B:
                        if b:
                            pe.wait_ge(skipped, 2 * b)
                        for m in range(2):
                            for c in range(2):
                                last = pe.matmul(ps_y[:, m, c * CH:(c + 1) * CH],
                                                 CT_sb[32 * b:32 * b + 32, m * 128:(m + 1) * 128],
                                                 hs[32 * b:32 * b + 32, 1 + c * CH:1 + (c + 1) * CH], start=True, stop=True)
                            last.then_inc(read, 1)
                    if b >= 1:
                        p = b - 1
                        pe.wait_ge(gated, 2 * b)
                        if p >= 2:
                            pe.wait_ge(biased, p - 1)
                        for c in range(2):
                            for m in range(2):
                                last = pe.matmul(ps_o[:, p % 2, c * CH:(c + 1) * CH], Wout_sb[:, m, :],
                                                 xconv[:, m, batch(p, c)], start=(m == 0), stop=(m == 1))
                        last.then_inc(out_ready, 1)

            @block.scalar
            def _(act):
                for b in range(B):
                    act.wait_ge(out_ready, b + 1)
                    if b >= 2:
                        act.wait_ge(added, b - 1)
                    act.activation(o[:, b % 2, :], ps_o[:, b % 2, :], ACT.Identity, bias=S.vec("b_out")).then_inc(biased, 1)

            @block.vector
            def _(dve):
                for b in range(B + 1):
                    if b < B:
                        for m in range(2):
                            dve.wait_ge(read, 2 * b + m + 1)
                            dve.scalar_tensor_tensor(out=xconv[:, m, batch(b)], in0=xconv[:, m, batch(b)], scalar=S.vec("Dp", m),
                                                     in1=ps_y[:, m, :], op0=ALU.mult, op1=ALU.add).then_inc(skipped, 1)
                        for m in range(2):
                            dve.wait_ge(skipped, 2 * b + m + 1)
                            dve.tensor_tensor(xconv[:, m, batch(b)], xconv[:, m, batch(b)], sz[:, m, batch(b)],
                                              ALU.mult).then_inc(gated, 1)
                    if b >= 1:
                        p = b - 1
                        dve.wait_ge(biased, b)
                        dve.scalar_tensor_tensor(out=S.xT[:, batch(p)], in0=o[:, p % 2, :], scalar=S.mod[:, 0, 2, p:p + 1],
                                                 in1=S.xT[:, batch(p)], op0=ALU.mult, op1=ALU.add).then_inc(added, 1)


def project_latent(nc, S, A, xn):
    NVT = T // 256
    items = ["latent", "k_turn_a", "k_turn_b"] + [f"k{g}" for g in range(NG)] + [f"v{v}" for v in range(NVT)]
    for g in range(NG):
        items += [f"q{g}", f"q_turn_a{g}", f"q_turn_b{g}"]
    SLOTS, NI = 4, len(items)
    units = [("kr", 32)] + [(f"k{g}", 128) for g in range(NG)]
    for g in range(NG):
        units += [(f"q{g}", 128), (f"r{g}", 128)]
    NU = len(units)
    rotations = [u for u in range(NU) if units[u][0] == "kr" or units[u][0][0] == "r"]
    NR = len(rotations)
    unit_of = {name: u for u, (name, _) in enumerate(units)}
    turn_items = {u: ("k_turn_a", "k_turn_b") if units[u][0] == "kr" else
                  (f"q_turn_a{units[u][0][1]}", f"q_turn_b{units[u][0][1]}") for u in rotations}
    stores_before = [sum(p % 2 == u % 2 for p in range(u)) for u in range(NU)]
    stores_of = [sum(p % 2 == s for p in range(NU)) for s in range(2)]
    with stage(nc) as ctx:
        def sb(name, shape, dt=F32):
            return ctx.enter_context(nc.sbuf_tensor(name, shape, dt))

        def sem(name):
            return semaphore(nc, ctx, "p0_" + name)

        Wn, Wr, Wrs = sb("Wq_n", [D, 512]), sb("Wq_r", [D, 512]), sb("Wq_rs", [D, 512])
        Wl, Wk, Wks, Wb = sb("Wkv_l", [D, 16]), sb("Wk_r0", [D, 32]), sb("Wk_r0s", [D, 32]), sb("Wkvb", [16, 512])
        cos, sin = sb("cos0", [128, T]), sb("sin0", [128, T])
        latent = sb("latent", [16, T])
        v_staged = [sb(f"v_staged{i}", [128, 2, H, 33]) for i in range(2)]
        parts = [sb(f"parts{i}", [128, 3, T], BF16) for i in range(2)]
        rest = [sb(f"rest{i}", [128, T]) for i in range(2)]
        turned = [sb(f"turned{i}", [128, 2, T]) for i in range(2)]
        whole = [sb(f"whole{i}", [128, T]) for i in range(2)]
        ps = [ctx.enter_context(nc.psum_tensor(f"ps_p0_{s}", [128, T], F32)) for s in range(SLOTS)]
        loaded, made, latent_kept, v_kept, ones_set = [sem(x) for x in ("loaded", "made", "latent_kept", "v_kept", "ones_set")]
        turned_a, turned_b, summed = sem("turned_a"), sem("turned_b"), sem("summed")
        part1, rest1, part2, part3 = sem("part1"), sem("rest1"), sem("part2"), sem("part3")
        v_stored, stored = [sem("v_stored0"), sem("v_stored1")], [sem("stored0"), sem("stored1")]
        block = ctx.enter_context(nc.Block())

        def ready(b, x):
            return b * NI + (items.index(x) + 1)

        def source(u):
            name = units[u][0]
            return whole[rotations.index(u) % 2] if u in rotations else ps[items.index(name) % SLOTS]

        @block.sync
        def _(sp):
            for to, x in ((Wn, "Wq_n"), (Wr, "Wq_r"), (Wrs, "Wq_rs"), (Wl, "Wkv_l"), (Wk, "Wk_r0"), (Wks, "Wk_r0s"),
                          (Wb, "Wkvb"), (cos, "cos0"), (sin, "sin0")):
                sp.dma_start(to[:, :], A[x]).then_inc(loaded, 16)
            with sp.Fori(0, B) as b:
                for u, (name, P) in enumerate(units):
                    sp.wait_ge(part3, b * NU + (u + 1))
                    g = 0 if name == "kr" else int(name[1])
                    to = {"k": S.k0[bass.ds(b, 1), g], "q": S.q0[bass.ds(b, 1), g, 0], "r": S.q0[bass.ds(b, 1), g, 1]}[name[0]] \
                        if name != "kr" else S.kr0[bass.ds(b, 1)]
                    sp.dma_start(to.rearrange("o n p t -> p (o n) t"), parts[u % 2][0:P, :, :]).then_inc(stored[u % 2], 16)
            for s in range(2):
                sp.wait_ge(stored[s], 16 * (B * stores_of[s] + 1))

        @block.tensor
        def _(pe):
            pe.wait_ge(loaded, 16 * 9)
            with pe.Fori(0, B) as b:
                for n, x in enumerate(items):
                    slot = ps[n % SLOTS]
                    if n >= SLOTS:
                        old = items[n - SLOTS]
                        if old == "latent":
                            pe.wait_ge(latent_kept, b + 1)
                        elif old[0] == "v":
                            pe.wait_ge(v_kept, b * NVT + (int(old[1]) + 1))
                        elif "turn" in old:
                            r = [r for r, u in enumerate(rotations) if old in turn_items[u]][0]
                            pe.wait_ge(turned_a if "_a" in old else turned_b, b * NR + (r + 1))
                        else:
                            pe.wait_ge(rest1, b * NU + (unit_of[old] + 1))
                    g = int(x[-1]) if x[-1].isdigit() else 0
                    cols = slice(g * 128, (g + 1) * 128)
                    if x[0] == "v":
                        for t in range(2):
                            tok = (2 * g + t) * 128
                            last = pe.matmul(slot[:, t * CH:(t + 1) * CH], latent[:, tok:tok + 128], Wb[:, :], start=True, stop=True)
                    elif x[0] == "k" and "turn" not in x:
                        pe.wait_ge(latent_kept, b + 1)
                        for c in range(2):
                            last = pe.matmul(slot[:, c * CH:(c + 1) * CH], Wb[:, cols], latent[:, c * CH:(c + 1) * CH],
                                             start=True, stop=True)
                    else:
                        w = {"latent": Wl, "k_turn_a": Wk, "k_turn_b": Wks}.get(x)
                        if w is None:
                            w = {"q": Wn, "q_turn_a": Wr, "q_turn_b": Wrs}[x[:-1]][:, cols]
                        else:
                            w = w[:, :]
                        M = w.shape[1]
                        for c in range(2):
                            last = pe.matmul(slot[0:M, c * CH:(c + 1) * CH], w, xn[:, bass.ds(b * T + c * CH, CH)],
                                             start=True, stop=True)
                    last.then_inc(made, 1)
                pe.wait_ge(rest1, b * NU + NU)
                pe.wait_ge(turned_b, b * NR + NR)
                pe.wait_ge(v_kept, b * NVT + NVT)

        @block.scalar
        def _(act):
            act.wait_ge(ones_set, 2)
            for s in range(2):
                act.sem_inc(stored[s], 16)
                act.sem_inc(v_stored[s], 16)
            with act.Fori(0, B) as b:
                act.wait_ge(made, ready(b, "latent"))
                act.activation(latent[:, :], ps[0][0:16, :], ACT.Identity).then_inc(latent_kept, 1)
                for u in range(NU + 1):
                    if u < NU:
                        name, P = units[u]
                        act.wait_ge(stored[u % 2], (b * stores_of[u % 2] + (stores_before[u] + 1)) * 16)
                        if u in rotations:
                            act.wait_ge(summed, b * NR + (rotations.index(u) + 1))
                        else:
                            act.wait_ge(made, ready(b, name))
                        act.activation(parts[u % 2][0:P, 0, :], source(u)[0:P, :], ACT.Identity).then_inc(part1, 1)
                    if u >= 1:
                        P = units[u - 1][1]
                        act.wait_ge(rest1, b * NU + u)
                        act.activation(parts[(u - 1) % 2][0:P, 1, :], rest[(u - 1) % 2][0:P, :], ACT.Identity).then_inc(part2, 1)
                    v = u - 2
                    if 0 <= v < NVT:
                        act.wait_ge(made, ready(b, f"v{v}"))
                        act.wait_ge(v_stored[v % 2], (b * 4 + (2 * (v // 2) + 1)) * 16)
                        act.activation(v_staged[v % 2][:, :, :, 0:32],
                                       ps[items.index(f"v{v}") % SLOTS][:, :].rearrange("p (t h d) -> p t h d", t=2, d=32),
                                       ACT.Identity).then_inc(v_kept, 1)
                        act.wait_ge(v_kept, b * NVT + (v + 1))
                        for t in range(2):
                            act.dma_start(S.v0[bass.ds(b, 1), 2 * v + t].rearrange("o p n -> (o p) n"),
                                          v_staged[v % 2][:, t, :, :].rearrange("p h d -> p (h d)")).then_inc(v_stored[v % 2], 16)
            for s in range(2):
                act.wait_ge(v_stored[s], 16 * (B * 4 + 1))

        @block.vector
        def _(dve):
            dve.wait_ge(loaded, 16 * 9)
            with dve.Fori(0, B) as b:
                def rotate(u):
                    r, P = rotations.index(u), units[u][1]
                    if r >= 2:
                        dve.wait_ge(summed, b * NR + (r - 1))
                    for j, (x, table, done) in enumerate(zip(turn_items[u], (cos, sin), (turned_a, turned_b))):
                        dve.wait_ge(made, ready(b, x))
                        dve.tensor_tensor(turned[r % 2][0:P, j, :], ps[items.index(x) % SLOTS][0:P, :], table[0:P, :],
                                          ALU.mult).then_inc(done, 1)

                rotate(0)
                for u in range(NU):
                    if u + 1 in rotations:
                        rotate(u + 1)
                    P = units[u][1]
                    dve.wait_ge(part1, b * NU + (u + 1))
                    if u >= 2:
                        dve.wait_ge(part3, b * NU + (u - 1))
                    dve.tensor_tensor(rest[u % 2][0:P, :], source(u)[0:P, :], parts[u % 2][0:P, 0, :], ALU.subtract)\
                       .then_inc(rest1, 1)
                dve.wait_ge(part3, b * NU + NU)
                dve.wait_ge(summed, b * NR + NR)

        @block.gpsimd
        def _(pool):
            pool.memset(v_staged[0][:, :, :, 32:33], 1.0).then_inc(ones_set, 1)
            pool.memset(v_staged[1][:, :, :, 32:33], 1.0).then_inc(ones_set, 1)
            with pool.Fori(0, B) as b:
                for u in range(-1, NU):
                    if u + 1 in rotations:
                        r, P = rotations.index(u + 1), units[u + 1][1]
                        pool.wait_ge(turned_b, b * NR + (r + 1))
                        if r >= 2:
                            pool.wait_ge(rest1, b * NU + (rotations[r - 2] + 1))
                        pool.tensor_tensor(whole[r % 2][0:P, :], turned[r % 2][0:P, 0, :], turned[r % 2][0:P, 1, :], ALU.add)\
                            .then_inc(summed, 1)
                    if u >= 0:
                        P = units[u][1]
                        pool.wait_ge(part2, b * NU + (u + 1))
                        pool.tensor_tensor(parts[u % 2][0:P, 2, :], rest[u % 2][0:P, :], parts[u % 2][0:P, 1, :], ALU.subtract)\
                            .then_inc(part3, 1)


def attention(nc, S, A, L):
    M, KT, NGR = L.hd + 1, T // 128, B * NG
    causal = L.causal
    steps = []
    for c in range(2):
        for kt in range(4 * c + 4 if causal else KT):
            q0 = max(c * CH, kt * 128) if causal else c * CH
            steps += [(c, kt, p, q0, (c + 1) * CH - q0) for p in range(2)]
    NSTEP, NPV = len(steps), len(steps) // 2
    first_chunk_pvs = sum(s[0] == 0 for s in steps) // 2
    tiles = []
    for qt in range(KT):
        keys = (qt + 1) * 128 if causal else T
        tiles += [(qt, j, lo, min(CH, keys - lo)) for j in range(HG) for lo in range(0, keys, CH)]
    NM = len(tiles)
    made_by = [0 if s < L.max_from else min(NM, -(-(s - L.max_from + 1) * NM // (L.max_to - L.max_from))) for s in range(NSTEP)]
    assert made_by[-1] == NM
    PR = 4
    MP = 3 * HG
    NCOPY = L.m_copies
    NO = L.o_banks
    NB = 4 - NO
    ST_CREDIT, PV_CREDIT = 2, 2
    with stage(nc) as ctx:
        def sb(name, shape, dt=F32):
            return ctx.enter_context(nc.sbuf_tensor(L.name + name, shape, dt))

        def sem(name):
            return semaphore(nc, ctx, L.name + name)

        Q = [sb(f"Q{i}", [128, HG, L.nq, T], BF16) for i in range(2)]
        K = [sb(f"K{i}", [128, HG, L.nk, T], BF16) for i in range(2)]
        V = [sb(f"V{i}", [128, KT, HG * M]) for i in range(2)]
        P = [sb(f"P{i}", [128, 2, CH]) for i in range(PR)]
        staged = [sb(f"staged{i}", [128, NO, CH]) for i in range(2)]
        m_half = sb("m_half", [128, KT, HG, 2])
        m_neg = sb("m_neg", [128, KT, HG])
        m_rest = sb("m_rest", [128, 2, KT, HG])
        m_parts = sb("m_parts", [128, KT, HG, 3], BF16)
        sel_col = sb("sel_col", [128, HG])
        if causal:
            mask_f, mask = sb("mask_f", [128, 2, 128]), sb("mask", [128, 2, 128], BF16)
            sel = sb("sel", [128, HG, 128], BF16)
            m_rows = [sb(f"m_rows{i}", [128, T], BF16) for i in range(2)]
        ps_st = [ctx.enter_context(nc.psum_tensor(f"{L.name}ps_st{i}", [128, 2, CH], F32)) for i in range(2)]
        ps_max = ctx.enter_context(nc.psum_tensor(L.name + "ps_max", [128, NB, CH], F32))
        ps_o = ctx.enter_context(nc.psum_tensor(L.name + "ps_o", [128, NO, CH], F32))
        m_turned = ps_max[L.m_row:L.m_row + MP, 0, :].bitcast(BF16)

        consts_loaded, cleared, consts_ready = sem("consts_loaded"), sem("cleared"), sem("consts_ready")
        loads = [sem("loads0"), sem("loads1")]
        st_ready, exp_done, pv_done = sem("st_ready"), sem("exp_done"), sem("pv_done")
        max_ready, reduced, m_split, m_chain = sem("max_ready"), sem("reduced"), sem("m_split"), sem("m_chain")
        m_rows_ready, m_copied = sem("m_rows_ready"), sem("m_copied")
        o_kept, o_stored = sem("o_kept"), [sem("o_stored0"), sem("o_stored1")]
        NLOAD, NSTORE = L.n_loads, L.n_stores

        with nc.Block() as block:
            @block.sync
            def _(sp):
                sp.dma_start(sel_col[:, :], A[L.sel]).then_inc(consts_loaded, 16)
                if causal:
                    sp.dma_start(mask_f[:, 0, :], A["mask"]).then_inc(consts_loaded, 16)
                    sp.dma_start(mask_f[:, 1, :], A["maskT"]).then_inc(consts_loaded, 16)

            @block.gpsimd
            def _(pool):
                if causal:
                    for i in range(2):
                        pool.memset(m_rows[i][:, :], 0.0)
                else:
                    for i in range(2):
                        pool.memset(Q[i][64:128, :, :, :], 0.0)
                        pool.memset(K[i][64:96, :, :, :], 0.0)

            @block.vector
            def _(dve):
                dve.memset(ps_o[:, :, :], 0.0)
                dve.wait_ge(consts_loaded, 48 if causal else 16)
                if causal:
                    dve.tensor_copy(mask[:, :, :], mask_f[:, :, :])
                    dve.tensor_copy(sel[:, :, :], sel_col[:, :].unsqueeze(2).broadcast_to([128, HG, 128]))
                else:
                    for i in range(2):
                        dve.tensor_copy(K[i][96:128, :, 0, :], sel_col[96:128, :].unsqueeze(2).broadcast_to([32, HG, T]))

        block = ctx.enter_context(nc.Block())

        def iterate(eng, body):
            with eng.Fori(0, NGR // 2 - 1) as i:
                body(i, 0, False)
                body(i, 1, False)
            body(NGR // 2 - 1, 0, False)
            body(NGR // 2 - 1, 1, True)

        @block.sync
        def _(sp):
            L.load(sp, 0, Q[0], K[0], V[0], loads[0])

            def body(i, par, last):
                n = i * 2 + par
                if not last:
                    sp.wait_ge(pv_done, n * NPV + PV_CREDIT)
                    L.load(sp, n + 1, Q[1 - par], K[1 - par], V[1 - par], loads[1 - par])
                for c in range(2):
                    sp.wait_ge(o_kept, n * 2 + (c + 2))
                    L.store(sp, n, c, staged[c], o_stored[c])

            iterate(sp, body)
            for c in range(2):
                sp.wait_ge(o_stored[c], 16 * (NSTORE * NGR + 1))

        @block.tensor
        def _(pe):
            pe.sem_inc(pv_done, PV_CREDIT)
            pe.sem_inc(m_rows_ready, 1)

            def maxima(g, par, t, first=False):
                qt, j, lo, w = tiles[t]
                if first and t >= NB:
                    pe.wait_ge(reduced, t + 1 - NB)
                if not first:
                    pe.wait_ge(reduced, g * NM + (max(0, t + 1 - NB)))
                if not first and t == 0:
                    pe.wait_ge(m_copied, g * NCOPY)
                to = ps_max[:, t % NB, 0:w]
                for x, (ks, qs) in enumerate(L.max_terms):
                    last = pe.matmul(to, Q[par][0:L.max_rows, j, qs, qt * 128:(qt + 1) * 128],
                                     K[par][0:L.max_rows, j, ks, lo:lo + w], start=(x == 0), stop=(x == len(L.max_terms) - 1))
                    if causal and x == 0 and lo + w == (qt + 1) * 128:
                        pe.matmul(ps_max[:, t % NB, w - 128:w], S.ident_bf[:, :], mask[:, 0, :], start=False, stop=False)
                last.then_inc(max_ready, 1)

            def turn_maxima(g):
                pe.wait_ge(m_split, g + 1)
                for qt in range(KT):
                    last = pe.transpose(m_turned[:, qt * 128:(qt + 1) * 128], m_parts[:, qt, :, :], S.ident_bf[:, :])
                last.then_inc(m_rows_ready, 1)

            def scores(n, par, s):
                c, kt, p, q0, w = steps[s]
                pe.wait_ge(exp_done, n * NSTEP + s + 1)
                if s == 0:
                    pe.wait_ge(m_copied, (n + 1) * NCOPY)
                for a in range(2):
                    j = 2 * p + a
                    out = ps_st[s % 2][:, a, :]
                    terms = [(K[par][:, j, ks, kt * 128:(kt + 1) * 128], Q[par][:, j, qs, q0:q0 + w]) for ks, qs in L.terms]
                    if causal:
                        terms.append((sel[:, j, :], m_rows[par][:, q0:q0 + w]))
                    for x, (lhsT, rhs) in enumerate(terms):
                        last = pe.matmul(out[:, 0:w], lhsT, rhs, start=(x == 0), stop=(x == len(terms) - 1))
                        if causal and x == 0 and q0 == kt * 128:
                            pe.matmul(out[:, 0:128], S.ident_bf[:, :], mask[:, 1, :], start=False, stop=False)
                last.then_inc(st_ready, 1)

            def values(n, par, k):
                c, kt, _, q0, w = steps[2 * k]
                pe.wait_ge(exp_done, n * NSTEP + (2 * k + 2) + ST_CREDIT)
                if kt == 0:
                    pe.wait_ge(o_kept, n * 2 + (c + 1))
                final = k + 1 == NPV or steps[2 * k + 2][0] != c
                for j in range(HG):
                    bank, row = L.o_place(j)
                    last = pe.matmul(ps_o[row:row + M, bank, q0 - c * CH:q0 - c * CH + w], V[par][:, kt, j * M:(j + 1) * M],
                                     P[(2 * k + j // 2) % PR][:, j % 2, 0:w], start=(kt == 0), stop=final)
                last.then_inc(pv_done, 1)

            pe.wait_ge(loads[0], 16 * NLOAD)
            for t in range(NM):
                maxima(0, 0, t, first=True)
            turn_maxima(0)

            def body(i, par, last):
                n = i * 2 + par
                t = k = 0
                for s in range(NSTEP):
                    scores(n, par, s)
                    while not last and t < made_by[s]:
                        if t == 0:
                            pe.wait_ge(loads[1 - par], (i + (1 + par)) * (16 * NLOAD))
                        maxima(n + 1, 1 - par, t)
                        t += 1
                    if not last and s == L.turn_at:
                        turn_maxima(n + 1)
                    if s % 2 and s >= 3:
                        values(n, par, k)
                        k += 1
                values(n, par, k)

            iterate(pe, body)

        @block.scalar
        def _(act):
            act.sem_inc(exp_done, ST_CREDIT)
            act.sem_inc(o_kept, 1)
            for c in range(2):
                act.sem_inc(o_stored[c], 16)

            def copy_rows(g, par, copy):
                if copy == 0:
                    act.wait_ge(m_rows_ready, g + 2)
                to = m_rows[par][0:MP, :] if causal else Q[par][L.m_row:L.m_row + MP, copy, 0, :]
                act.activation(to, m_turned, ACT.Identity).then_inc(m_copied, 1)

            def keep(n, c):
                act.wait_ge(pv_done, n * NPV + ((NPV if c else first_chunk_pvs) + PV_CREDIT))
                act.wait_ge(o_stored[c], n * (16 * NSTORE) + 16)
                L.keep(act, staged[c], ps_o, o_kept)

            for copy in range(NCOPY):
                copy_rows(0, 0, copy)

            def body(i, par, last):
                n = i * 2 + par
                for s in range(NSTEP):
                    act.wait_ge(st_ready, n * NSTEP + (s + 1))
                    act.wait_ge(pv_done, n * NPV + (s // 2 + 1))
                    w = steps[s][4]
                    act.activation(P[s % PR][:, :, 0:w], ps_st[s % 2][:, :, 0:w], ACT.Exp, scale=L.scale).then_inc(exp_done, 1)
                    if s == 2 * first_chunk_pvs + 3:
                        keep(n, 0)
                    copy = s - L.turn_at - 1
                    if not last and 0 <= copy < NCOPY:
                        copy_rows(n + 1, 1 - par, copy)
                if not last:
                    for copy in range(NSTEP - L.turn_at - 1, NCOPY):
                        copy_rows(n + 1, 1 - par, copy)
                keep(n, 1)

            iterate(act, body)

        @block.vector
        def _(dve):
            LINKS = 4

            def group_maxima(g):
                for t, (qt, j, lo, w) in enumerate(tiles):
                    dve.wait_ge(max_ready, g * NM + (t + 1))
                    dve.tensor_reduce(m_half[:, qt, j, lo // CH:lo // CH + 1], ps_max[:, t % NB, 0:w], AX.X, ALU.max, negate=True)\
                       .then_inc(reduced, 1)
                dve.wait_ge(reduced, g * NM + NM)
                dve.tensor_tensor(m_neg[:, :, :], m_half[:, :, :, 0], m_half[:, :, :, 1], ALU.min).then_inc(m_chain, 1)
                dve.wait_ge(m_chain, g * LINKS + 1)
                dve.wait_ge(m_rows_ready, g + 1)
                dve.tensor_copy(m_parts[:, :, :, 0], m_neg[:, :, :]).then_inc(m_chain, 1)
                dve.wait_ge(m_chain, g * LINKS + 2)
                dve.tensor_tensor(m_rest[:, 0, :, :], m_neg[:, :, :], m_parts[:, :, :, 0], ALU.subtract).then_inc(m_chain, 1)
                dve.wait_ge(m_chain, g * LINKS + 3)
                dve.tensor_copy(m_parts[:, :, :, 1], m_rest[:, 0, :, :]).then_inc(m_chain, 1)
                dve.wait_ge(m_chain, g * LINKS + 4)
                dve.tensor_tensor(m_parts[:, :, :, 2], m_rest[:, 0, :, :], m_parts[:, :, :, 1], ALU.subtract).then_inc(m_split, 1)
                dve.wait_ge(m_split, g + 1)

            dve.memset(m_half[:, :, :, :], -NEG)
            dve.drain()
            with dve.Fori(0, NGR) as g:
                group_maxima(g)


def latent_layer():
    L = State()
    L.name, L.causal, L.hd, L.scale, L.sel = "a0_", True, 32, 0.125, "sel0"
    L.nq, L.nk, L.o_banks, L.m_row, L.m_copies = 2, 3, 2, 0, 1
    L.terms = [(0, 0), (1, 0), (2, 1)]
    L.max_terms, L.max_rows = [(0, 0), (1, 0)], 128
    L.max_from, L.max_to, L.turn_at = 11, 24, 23
    L.o_place = lambda j: (j // 2, 64 * (j % 2))
    return L


def latent_attention(nc, S, A):
    S.q0 = nc.dram_tensor("q0_parts", [B, NG, 2, 3, 128, T], BF16).ap()
    S.k0 = nc.dram_tensor("k0_parts", [B, NG, 3, 128, T], BF16).ap()
    S.kr0 = nc.dram_tensor("kr0_parts", [B, 3, 32, T], BF16).ap()
    S.v0 = nc.dram_tensor("v0_rows", [B, T // 128, 128, H * 33], F32).ap()
    S.o0 = nc.dram_tensor("o0_heads", [H, 32, N], F32).ap()
    S.sum0 = nc.dram_tensor("sum0_heads", [H, N], F32).ap()
    with stage(nc) as ctx:
        xn = ctx.enter_context(nc.sbuf_tensor("xn0", [D, N], F32))
        rmsnorm(nc, S, S.hT, xn, "ln1", "rms1")
        project_latent(nc, S, A, xn)
    L = latent_layer()
    L.n_loads, L.n_stores = 8 + 6 + 6 + 1, 4

    def load(sp, n, Q, K, V, done):
        b, g = n // NG, n % NG
        q = S.q0[bass.ds(b, 1), bass.ds(g, 1)].rearrange("b g k n (h r) t -> k n r (b g h) t", r=32)
        k = S.k0[bass.ds(b, 1), bass.ds(g, 1)].rearrange("b g n (h r) t -> n r (b g h) t", r=32)
        kr = S.kr0[bass.ds(b, 1)].rearrange("b n r t -> n r b t")
        for s, halves in enumerate(((0, 1), (2, 0))):
            for half, part in enumerate(halves):
                for kind in range(2):
                    lo = 64 * half + 32 * kind
                    sp.dma_start(Q[lo:lo + 32, :, s, :], q[kind, part]).then_inc(done, 16)
        for s, halves in enumerate(((0, 0), (1, 1), (0, 2))):
            for half, part in enumerate(halves):
                sp.dma_start(K[64 * half:64 * half + 32, :, s, :], k[part]).then_inc(done, 16)
                sp.dma_start(K[64 * half + 32:64 * half + 64, :, s, :], kr[part].broadcast_to([32, HG, T])).then_inc(done, 16)
        sp.dma_start(V[:, :, :], S.v0[bass.ds(b, 1), :, :, bass.ds(g * (HG * 33), HG * 33)].rearrange("b k p n -> p (b k) n"))\
          .then_inc(done, 16)

    def store(sp, n, c, staged, done):
        b, g = n // NG, n % NG
        cols = bass.ds(b * T + c * CH, CH)
        for a in range(2):
            to = S.o0[bass.ds(g * HG, HG), :, cols].rearrange("(p a) r t -> a r p t", a=2)
            sp.dma_start(to[a], staged[64 * a:64 * a + 32, :, :]).then_inc(done, 16)
            to = S.sum0[bass.ds(g * HG, HG), cols].rearrange("(o p a) t -> a o p t", a=2, o=1)
            sp.dma_start(to[a], staged[64 * a + 32:64 * a + 33, :, :]).then_inc(done, 16)

    def keep(act, staged, ps_o, kept):
        act.activation(staged[0:97, :, :], ps_o[0:97, :, :], ACT.Identity).then_inc(kept, 1)

    L.load, L.store, L.keep = load, store, keep
    attention(nc, S, A, L)
    merge_heads(nc, S, A, 0)


def merge_heads(nc, S, A, l):
    NT = 4 if l == 0 else 1
    o, sums = (S.o0, S.sum0) if l == 0 else (S.o1, S.sum1)
    with stage(nc) as ctx:
        def sb(name, shape, dt=F32):
            return ctx.enter_context(nc.sbuf_tensor(f"mh{l}_{name}", shape, dt))

        def sem(name):
            return semaphore(nc, ctx, f"mh{l}_{name}")

        y, Wo = sb("y", [128, NT, N]), sb("Wo", [128, NT, D])
        flat, inv = sb("flat", [128, H * N // 128]), sb("inv", [H, N])
        pick = sb("pick", [H, NT, 128])
        biased = sb("biased", [D, 2, T])
        ps_s = ctx.enter_context(nc.psum_tensor(f"mh{l}_ps_s", [128, 2, T], F32))
        ps_o = ctx.enter_context(nc.psum_tensor(f"mh{l}_ps_o", [128, 2, T], F32))
        inv_dram = nc.dram_tensor(f"inverse_sums{l}", [H, N], F32).ap()
        loaded, flat_loaded, inverted, inv_stored, inv_loaded = [sem(x) for x in ("loaded", "flat", "inverted", "inv_stored", "inv_loaded")]
        spread, divided, projected, bias_added, added = [sem(x) for x in ("spread", "divided", "projected", "bias_added", "added")]
        block = ctx.enter_context(nc.Block())

        @block.sync
        def _(sp):
            sp.dma_start(flat[:, :], sums.rearrange("h (x t) -> (h x) t", x=128 // H)).then_inc(flat_loaded, 16)
            sp.dma_start(Wo[:, :, :], A[f"Wo{l}"].rearrange("(n p) d -> p n d", p=128)).then_inc(loaded, 16)
            sp.dma_start(pick[:, :, :], A[f"pick{l}"].rearrange("h (n p) -> h n p", p=128)).then_inc(loaded, 16)
            for n in range(NT):
                sp.dma_start(y[:, n, :], o.rearrange("h r t -> (h r) t")[n * 128:(n + 1) * 128, :]).then_inc(loaded, 16)
            sp.wait_ge(inverted, 1)
            sp.dma_start(inv_dram.rearrange("h (x t) -> (h x) t", x=128 // H), flat[:, :]).then_inc(inv_stored, 16)
            sp.wait_ge(inv_stored, 16)
            sp.dma_start(inv[:, :], inv_dram).then_inc(inv_loaded, 16)

        @block.tensor
        def _(pe):
            pe.wait_ge(loaded, 16 * (2 + NT))
            pe.wait_ge(inv_loaded, 16)
            for u in range(B * NT + NT):
                if u < B * NT:
                    b, n = u // NT, u % NT
                    if u >= 2:
                        pe.wait_ge(divided, u - 1)
                    for c in range(2):
                        last = pe.matmul(ps_s[:, u % 2, c * CH:(c + 1) * CH], pick[:, n, :], inv[:, batch(b, c)],
                                         start=True, stop=True)
                    last.then_inc(spread, 1)
                if u >= NT and u % NT == NT - 1:
                    b = u // NT - 1
                    pe.wait_ge(divided, (b + 1) * NT)
                    if b >= 2:
                        pe.wait_ge(bias_added if l else added, b - 1)
                    for c in range(2):
                        for n in range(NT):
                            last = pe.matmul(ps_o[:, b % 2, c * CH:(c + 1) * CH], Wo[:, n, :], y[:, n, batch(b, c)],
                                             start=(n == 0), stop=(n == NT - 1))
                    last.then_inc(projected, 1)

        @block.scalar
        def _(act):
            if l:
                for b in range(B):
                    act.wait_ge(projected, b + 1)
                    if b >= 2:
                        act.wait_ge(added, b - 1)
                    act.activation(biased[:, b % 2, :], ps_o[:, b % 2, :], ACT.Identity, bias=S.vec("Wo_b")).then_inc(bias_added, 1)

        @block.vector
        def _(dve):
            dve.wait_ge(flat_loaded, 16)
            dve.reciprocal(flat[:, :], flat[:, :]).then_inc(inverted, 1)
            dve.wait_ge(loaded, 16 * (2 + NT))
            for b in range(B + 1):
                if b < B:
                    for n in range(NT):
                        dve.wait_ge(spread, b * NT + n + 1)
                        dve.tensor_tensor(y[:, n, batch(b)], y[:, n, batch(b)], ps_s[:, (b * NT + n) % 2, :], ALU.mult).then_inc(divided, 1)
                if b >= 1:
                    p = b - 1
                    if l == 0:
                        dve.wait_ge(projected, b)
                        dve.tensor_tensor(S.hT[:, batch(p)], S.hT[:, batch(p)], ps_o[:, p % 2, :], ALU.add).then_inc(added, 1)
                    else:
                        dve.wait_ge(bias_added, b)
                        dve.scalar_tensor_tensor(out=S.xT[:, batch(p)], in0=biased[:, p % 2, :], scalar=S.mod[:, 1, 2, p:p + 1],
                                                 in1=S.xT[:, batch(p)], op0=ALU.mult, op1=ALU.add).then_inc(added, 1)


def project_heads(nc, S, A):
    NI, TURNS = 8, 6
    A_, B_, U_ = 0, 1, 2
    with stage(nc) as ctx:
        def sb(name, shape, dt=F32):
            return ctx.enter_context(nc.sbuf_tensor("p1_" + name, shape, dt))

        def sem(name):
            return semaphore(nc, ctx, "p1_" + name)

        Wd, bd = sb("Wd", [D, 2, 64]), sb("bd", [128, 1])
        Wu = sb("Wu", [64, 3, D])
        Wk = sb("Wk", [D, 2, D])
        Wkv = sb("Wkv", [128, 2, D])
        bv, ones = sb("bv", [1, D]), sb("ones", [1, 128])
        cos, sin = sb("cos", [128, T]), sb("sin", [128, T])
        ct = sb("ct", [128, T])
        v_staged = sb("v_staged", [128, T // 128, H, 9])
        turned = [sb(f"turned{i}", [128, 2, T]) for i in range(2)]
        whole = [sb(f"whole{i}", [128, T]) for i in range(2)]
        rest = [sb(f"rest{i}", [128, T]) for i in range(2)]
        parts = [sb(f"parts{i}", [128, 3, T], BF16) for i in range(2)]
        ps = [ctx.enter_context(nc.psum_tensor(f"p1_ps{s}", [128, T], F32)) for s in range(4)]
        loaded, ones_set, made, ct_kept, turn, summed = [sem(x) for x in ("loaded", "ones", "made", "ct_kept", "turn", "summed")]
        part1, rest1, part2, part3 = sem("part1"), sem("rest1"), sem("part2"), sem("part3")
        v_kept, v_stored, stored = sem("v_kept"), sem("v_stored"), sem("stored")
        block = ctx.enter_context(nc.Block())

        @block.sync
        def _(sp):
            for to, x in ((Wd[:, 0, :], "Wd_q"), (Wd[:, 1, :], "Wd_kv"), (bd[0:64, :], "bd_q"), (bd[64:128, :], "bd_kv"),
                          (Wu[:, 0, :], "Wq_r1"), (Wu[:, 1, :], "Wq_r1s"), (Wu[:, 2, :], "Wu_q"), (Wk[:, 0, :], "Wk_r1"),
                          (Wk[:, 1, :], "Wk_r1s"), (Wkv[64:128, 0, :], "Wu_k"), (Wkv[64:128, 1, :], "Wu_v"), (bv[:, :], "bu_v"),
                          (cos[:, :], "cos1"), (sin[:, :], "sin1")):
                sp.dma_start(to, A[x]).then_inc(loaded, 16)
            with sp.Fori(0, B) as b:
                for u in range(2):
                    sp.wait_ge(part3, b * 2 + (u + 1))
                    to = (S.q1, S.k1)[u][bass.ds(b, 1)].rearrange("b n p t -> p (b n) t")
                    sp.dma_start(to, parts[u][:, :, :]).then_inc(stored, 16)
                sp.wait_ge(v_kept, b + 1)
                sp.dma_start(S.v1[bass.ds(b, 1)].rearrange("b k p n -> p (b k) n"),
                             v_staged[:, :, :, :].rearrange("p k h d -> p k (h d)")).then_inc(v_stored, 16)
            sp.wait_ge(stored, 32 * B + 16)
            sp.wait_ge(v_stored, 16 * B + 16)

        @block.tensor
        def _(pe):
            pe.wait_ge(loaded, 16 * 14)
            pe.wait_ge(ones_set, 2)
            with pe.Fori(0, B) as b:
                def product(s, w, x):
                    for c in range(2):
                        last = pe.matmul(ps[s][:, c * CH:(c + 1) * CH], w, x(c), start=True, stop=True)
                    last.then_inc(made, 1)

                def h(c):
                    return S.hT[:, bass.ds(b * T + c * CH, CH)]

                product(0, Wd[:, :, :].rearrange("d x i -> d (x i)"), h)
                pe.wait_ge(ct_kept, b + 1)
                product(1, Wu[:, 0, :], lambda c: ct[0:64, c * CH:(c + 1) * CH])
                product(2, Wu[:, 1, :], lambda c: ct[0:64, c * CH:(c + 1) * CH])
                product(3, Wu[:, 2, :], lambda c: ct[0:64, c * CH:(c + 1) * CH])
                product(0, Wk[:, 0, :], h)
                pe.wait_ge(turn, b * TURNS + 1)
                product(1, Wk[:, 1, :], h)
                pe.wait_ge(turn, b * TURNS + 2)
                product(2, Wkv[64:128, 0, :], lambda c: ct[64:128, c * CH:(c + 1) * CH])
                pe.wait_ge(turn, b * TURNS + 3)
                for t in range(T // 128):
                    pe.matmul(ps[3][:, t * 128:(t + 1) * 128], ct[64:128, t * 128:(t + 1) * 128], Wkv[64:128, 1, :],
                              start=True, stop=False)
                    last = pe.matmul(ps[3][:, t * 128:(t + 1) * 128], ones[:, :], bv[:, :], start=False, stop=True)
                last.then_inc(made, 1)
                pe.wait_ge(turn, b * TURNS + TURNS)
                pe.wait_ge(v_kept, b + 1)

        @block.scalar
        def _(act):
            act.wait_ge(loaded, 16 * 14)
            act.sem_inc(stored, 16)
            act.sem_inc(v_stored, 16)
            act.wait_ge(ones_set, 2)
            with act.Fori(0, B) as b:
                act.wait_ge(made, b * NI + 1)
                act.activation(ct[:, :], ps[0][:, :], ACT.Identity, bias=bd[:, 0:1]).then_inc(ct_kept, 1)
                act.wait_ge(stored, b * 32 + 16)
                for u in range(2):
                    act.wait_ge(summed, b * 2 + (u + 1))
                    act.activation(parts[u][:, 0, :], whole[u][:, :], ACT.Identity).then_inc(part1, 1)
                    if u == 0:
                        act.wait_ge(made, b * NI + NI)
                        act.wait_ge(v_stored, b * 16 + 16)
                        act.activation(v_staged[:, :, :, 0:8], ps[3][:, :].rearrange("p (k h d) -> p k h d", h=H, d=8),
                                       ACT.Identity).then_inc(v_kept, 1)
                    act.wait_ge(rest1, b * 2 + (u + 1))
                    act.activation(parts[u][:, 1, :], rest[u][:, :], ACT.Identity).then_inc(part2, 1)

        @block.vector
        def _(dve):
            dve.wait_ge(loaded, 16 * 14)
            with dve.Fori(0, B) as b:
                for u, (made_at, slots, biases) in enumerate((((2, 3, 4), (1, 2, 3), ("Wq_r_b", "Wq_r_bs", "Wu_q_b")),
                                                              ((5, 6, 7), (0, 1, 2), ("Wk_r_b", "Wk_r_bs", "Wu_k_b")))):
                    for j, table in ((A_, cos), (B_, sin)):
                        dve.wait_ge(made, b * NI + made_at[j])
                        dve.scalar_tensor_tensor(out=turned[u][:, j, :], in0=ps[slots[j]][:, :], scalar=S.vec(biases[j]),
                                                 in1=table[:, :], op0=ALU.add, op1=ALU.mult).then_inc(turn, 1)
                    dve.wait_ge(made, b * NI + made_at[U_])
                    dve.wait_ge(turn, b * TURNS + (3 * u + 1))
                    dve.scalar_tensor_tensor(out=whole[u][:, :], in0=ps[slots[U_]][:, :], scalar=S.vec(biases[U_]),
                                             in1=turned[u][:, A_, :], op0=ALU.add, op1=ALU.add).then_inc(turn, 1)
                for u in range(2):
                    dve.wait_ge(part1, b * 2 + (u + 1))
                    dve.tensor_tensor(rest[u][:, :], whole[u][:, :], parts[u][:, 0, :], ALU.subtract).then_inc(rest1, 1)
                dve.wait_ge(part3, b * 2 + 2)

        @block.gpsimd
        def _(pool):
            pool.memset(ones[:, :], 1.0).then_inc(ones_set, 1)
            pool.memset(v_staged[:, :, :, 8:9], 1.0).then_inc(ones_set, 1)
            with pool.Fori(0, B) as b:
                for u in range(2):
                    pool.wait_ge(turn, b * TURNS + (3 * u + 3))
                    pool.tensor_tensor(whole[u][:, :], whole[u][:, :], turned[u][:, B_, :], ALU.add).then_inc(summed, 1)
                for u in range(2):
                    pool.wait_ge(part2, b * 2 + (u + 1))
                    pool.tensor_tensor(parts[u][:, 2, :], rest[u][:, :], parts[u][:, 1, :], ALU.subtract).then_inc(part3, 1)


def head_attention(nc, S, A):
    S.q1 = nc.dram_tensor("q1_parts", [B, 3, 128, T], BF16).ap()
    S.k1 = nc.dram_tensor("k1_parts", [B, 3, 128, T], BF16).ap()
    S.v1 = nc.dram_tensor("v1_rows", [B, T // 128, 128, H * 9], F32).ap()
    S.o1 = nc.dram_tensor("o1_heads", [H, 8, N], F32).ap()
    S.sum1 = nc.dram_tensor("sum1_heads", [H, N], F32).ap()
    project_heads(nc, S, A)
    L = State()
    L.name, L.causal, L.hd, L.scale, L.sel = "a1_", False, 8, 1.0 / 12.0, "sel1"
    L.nq, L.nk, L.o_banks, L.m_row, L.m_copies = 1, 1, 1, 96, HG
    L.terms, L.max_terms, L.max_rows = [(0, 0)], [(0, 0)], 96
    L.max_from, L.max_to, L.turn_at = 10, 31, 31
    L.o_place = lambda j: (0, 32 * j)
    L.n_loads, L.n_stores = 19, 8

    def load(sp, n, Q, K, V, done):
        b, g = n // NG, n % NG
        rows = bass.ds(g * (HG * 8), HG * 8)
        q = S.q1[bass.ds(b, 1), :, rows].rearrange("b n (h r) t -> n r (b h) t", r=8)
        k = S.k1[bass.ds(b, 1), :, rows].rearrange("b n (h r) t -> n r (b h) t", r=8)
        for x in range(3):
            for y in range(3):
                lo = 24 * x + 8 * y
                sp.dma_start(Q[lo:lo + 8, :, 0, :], q[y]).then_inc(done, 16)
                sp.dma_start(K[lo:lo + 8, :, 0, :], k[x]).then_inc(done, 16)
        sp.dma_start(V[:, :, :], S.v1[bass.ds(b, 1), :, :, bass.ds(g * (HG * 9), HG * 9)].rearrange("b k p n -> p (b k) n"))\
          .then_inc(done, 16)

    def store(sp, n, c, staged, done):
        b, g = n // NG, n % NG
        cols = bass.ds(b * T + c * CH, CH)
        o, sums = S.o1[bass.ds(g * HG, HG), :, cols], S.sum1[bass.ds(g * HG, HG), cols]
        for j in range(HG):
            sp.dma_start(o[j], staged[32 * j:32 * j + 8, 0, :]).then_inc(done, 16)
            sp.dma_start(sums[j:j + 1], staged[32 * j + 8:32 * j + 9, 0, :]).then_inc(done, 16)

    def keep(act, staged, ps_o, kept):
        act.activation(staged[0:105, :, :], ps_o[0:105, :, :], ACT.Identity).then_inc(kept, 1)

    L.load, L.store, L.keep = load, store, keep
    attention(nc, S, A, L)
    merge_heads(nc, S, A, 1)


CAP = 320
NT = N // 128
X = 8


def route(nc, S, A, l, src, comb):
    R = X + 1 if l else X
    name = f"r{l}_"
    with stage(nc) as ctx:
        def sb(n, shape, dt=F32):
            return ctx.enter_context(nc.sbuf_tensor(name + n, shape, dt))

        def sem(n):
            return semaphore(nc, ctx, name + n)

        Wg, bias, number = sb("W", [D, X]), sb("bias", [128, X]), sb("number", [128, X])
        logits, work = sb("logits", [128, NT, X]), sb("work", [128, NT, X])
        hot = [sb(f"hot{i}", [128, NT, X]) for i in range(2)]
        top = [sb(f"top{i}", [128, NT]) for i in range(2)]
        low, e2, w = sb("low", [128, NT]), sb("e2", [128, NT]), sb("w", [128, 2, NT])
        weights = sb("weights", [128, NT, R])
        ps = ctx.enter_context(nc.psum_tensor(name + "ps", [128, NT, X], F32))
        ps_t = ctx.enter_context(nc.psum_tensor(name + "ps_t", [R, 2, T], F32))
        loaded, made, chain, diff, exped, weighed, turned, kept, elig_ready, offset_ready = [
            sem(x) for x in ("loaded", "made", "chain", "diff", "exped", "weighed", "turned", "kept", "elig", "offset")]
        if l:
            before, fb, elig, count, keep_, fits = (sb("before", [128, 128]), sb("fb", [128, NT]), sb("elig", [128, NT]),
                                                    sb("count", [128, NT]), sb("keep", [128, NT, X]), sb("fits", [128, NT]))
            ones = sb("ones", [128, NT])
            ps_off = ctx.enter_context(nc.psum_tensor(name + "ps_off", [128, 1], F32))
        block = ctx.enter_context(nc.Block())
        NLOAD = 3

        @block.sync
        def _(sp):
            sp.dma_start(Wg[:, :], A["Wr" if l else "Wgate"]).then_inc(loaded, 16)
            sp.dma_start(number[:, :], A["number"].partition_broadcast(128)).then_inc(loaded, 16)
            if l:
                sp.dma_start(before[:, :], A["before"]).then_inc(loaded, 16)
            else:
                sp.dma_start(bias[:, :], A["gate_b"].partition_broadcast(128)).then_inc(loaded, 16)

        @block.tensor
        def _(pe):
            pe.wait_ge(loaded, 16 * NLOAD)
            for t in range(NT):
                last = pe.matmul(ps[:, t, :], src[:, t:N:NT], Wg[:, :], start=True, stop=True)
            last.then_inc(made, 1)
            if l:
                for e in range(X):
                    pe.wait_ge(elig_ready, e + 1)
                    pe.matmul(ps_off[:, :], before[:, :], count[:, NT - 1:NT], start=True, stop=True).then_inc(offset_ready, 1)
            pe.wait_ge(weighed, 1)
            for q in range(B):
                if q >= 2:
                    pe.wait_ge(kept, q - 1)
                for t in range(8):
                    last = pe.transpose(ps_t[:, q % 2, t * 128:(t + 1) * 128], weights[:, q * 8 + t, :], S.ident[:, :])
                last.then_inc(turned, 1)

        @block.scalar
        def _(act):
            act.wait_ge(diff, 1)
            act.activation(e2[:, :], e2[:, :], ACT.Exp).then_inc(exped, 1)
            for q in range(B):
                act.wait_ge(turned, q + 1)
                to = comb[:, :].rearrange("r (p t) -> r t p", t=NT)[:, q * 8:(q + 1) * 8, :]
                act.activation(to, ps_t[:, q % 2, :].rearrange("r (t p) -> r t p", p=128), ACT.Identity).then_inc(kept, 1)

        @block.vector
        def _(dve):
            n = 0

            def link(ins):
                nonlocal n
                n += 1
                ins.then_inc(chain, 1)
                dve.wait_ge(chain, n)

            def over(x):
                return x.unsqueeze(2).broadcast_to([128, NT, X])

            def every(x):
                return x.unsqueeze(1).broadcast_to([128, NT, X])

            dve.wait_ge(loaded, 16 * NLOAD)
            dve.wait_ge(made, 1)
            if l:
                link(dve.tensor_copy(logits[:, :, :], ps[:, :, :]))
            else:
                link(dve.tensor_tensor(logits[:, :, :], ps[:, :, :], every(bias[:, :]), ALU.add))
            for k in range(2):
                link(dve.tensor_reduce(top[k][:, :], logits[:, :, :], AX.X, ALU.max))
                link(dve.tensor_tensor(work[:, :, :], logits[:, :, :], over(top[k][:, :]), ALU.is_equal))
                link(dve.scalar_tensor_tensor(out=work[:, :, :], in0=work[:, :, :], scalar=-float(X), in1=every(number[:, :]),
                                              op0=ALU.mult, op1=ALU.add))
                link(dve.tensor_reduce(low[:, :], work[:, :, :], AX.X, ALU.min))
                link(dve.tensor_tensor(hot[k][:, :, :], work[:, :, :], over(low[:, :]), ALU.is_equal))
                if k == 0:
                    link(dve.scalar_tensor_tensor(out=logits[:, :, :], in0=hot[0][:, :, :], scalar=2 * NEG, in1=logits[:, :, :],
                                                  op0=ALU.mult, op1=ALU.add))
            dve.tensor_tensor(e2[:, :], top[1][:, :], top[0][:, :], ALU.subtract).then_inc(diff, 1)
            dve.wait_ge(exped, 1)
            link(dve.tensor_scalar_add(w[:, 0, :], e2[:, :], 1.0))
            link(dve.reciprocal(w[:, 0, :], w[:, 0, :]))
            link(dve.tensor_tensor(w[:, 1, :], e2[:, :], w[:, 0, :], ALU.mult))
            if l:
                link(dve.tensor_tensor(work[:, :, :], hot[0][:, :, :], hot[1][:, :, :], ALU.add))
                link(dve.memset(fb[:, :], 0.0))
                link(dve.memset(ones[:, :], 1.0))
                for e in range(X):
                    link(dve.tensor_tensor(fits[:, :], ones[:, :], fb[:, :], ALU.subtract))
                    link(dve.tensor_tensor(elig[:, :], fits[:, :], work[:, :, e], ALU.mult))
                    dve.tensor_tensor_scan(count[:, :], ones[:, :], elig[:, :], 0.0, ALU.mult, ALU.add).then_inc(elig_ready, 1)
                    dve.wait_ge(offset_ready, e + 1)
                    link(dve.tensor_scalar(fits[:, :], count[:, :], ps_off[:, 0:1], float(CAP), ALU.add, ALU.is_le))
                    link(dve.tensor_tensor(keep_[:, :, e], fits[:, :], elig[:, :], ALU.mult))
                    link(dve.tensor_tensor(elig[:, :], elig[:, :], keep_[:, :, e], ALU.subtract))
                    link(dve.tensor_tensor(fb[:, :], fb[:, :], elig[:, :], ALU.add))
                link(dve.tensor_tensor(fits[:, :], ones[:, :], fb[:, :], ALU.subtract))
                link(dve.tensor_tensor(keep_[:, :, :], keep_[:, :, :], over(fits[:, :]), ALU.mult))
                link(dve.tensor_copy(weights[:, :, X:R], fb[:, :].unsqueeze(2)))
            link(dve.tensor_tensor(hot[0][:, :, :], hot[0][:, :, :], over(w[:, 0, :]), ALU.mult))
            link(dve.tensor_tensor(hot[1][:, :, :], hot[1][:, :, :], over(w[:, 1, :]), ALU.mult))
            link(dve.tensor_tensor(weights[:, :, 0:X], hot[0][:, :, :], hot[1][:, :, :], ALU.add))
            if l:
                link(dve.tensor_tensor(weights[:, :, 0:X], weights[:, :, 0:X], keep_[:, :, :], ALU.mult))
            dve.drain().then_inc(weighed, 1)


def gated_experts(nc, S, A, xn, comb):
    NC = N // CH
    NP = X // 2 + 1
    with stage(nc) as ctx:
        def sb(name, shape, dt=F32):
            return ctx.enter_context(nc.sbuf_tensor("g_" + name, shape, dt))

        def sem(name):
            return semaphore(nc, ctx, "g_" + name)

        Wg, Wu, Wd = sb("Wg", [D, NP, 128]), sb("Wu", [D, NP, 128]), sb("Wd", [128, NP, D])
        pick = sb("pick", [X, NP - 1, 128])
        act_g = [sb(f"act{i}", [128, CH]) for i in range(2)]
        prod = [sb(f"prod{i}", [128, CH]) for i in range(2)]
        ps_g = [ctx.enter_context(nc.psum_tensor(f"g_ps_g{i}", [128, CH], F32)) for i in range(2)]
        ps_u = [ctx.enter_context(nc.psum_tensor(f"g_ps_u{i}", [128, CH], F32)) for i in range(2)]
        ps_w = [ctx.enter_context(nc.psum_tensor(f"g_ps_w{i}", [128, CH], F32)) for i in range(2)]
        ps_o = ctx.enter_context(nc.psum_tensor("g_ps_o", [128, CH], F32))
        loaded, padded, made, gated, multiplied, weighted, summed, joined = [
            sem(x) for x in ("loaded", "padded", "made", "gated", "multiplied", "weighted", "summed", "joined")]
        block = ctx.enter_context(nc.Block())

        @block.gpsimd
        def _(pool):
            for x in (Wg, Wu, Wd):
                pool.memset(x[:, NP - 1, :], 0.0).then_inc(padded, 1)

        @block.sync
        def _(sp):
            for to, x in ((Wg, "Wg"), (Wu, "Wu")):
                sp.dma_start(to[:, 0:NP - 1, :].rearrange("p n (a i) -> p (n a) i", a=2), A[x].rearrange("e d i -> d e i")).then_inc(loaded, 16)
            sp.dma_start(Wd[:, 0:NP - 1, :], A["Wd"].rearrange("(n a) i d -> (a i) n d", a=2)).then_inc(loaded, 16)
            sp.wait_ge(padded, 3)
            for to, x in ((Wg[:, NP - 1, 0:64], "sWg"), (Wu[:, NP - 1, 0:64], "sWu"), (Wd[0:64, NP - 1, :], "sWd")):
                sp.dma_start(to, A[x][0]).then_inc(loaded, 16)
            sp.dma_start(pick[:, :, :], A["pick_e"].rearrange("e (n p) -> e n p", p=128)).then_inc(loaded, 16)

        @block.tensor
        def _(pe):
            pe.wait_ge(loaded, 16 * 7)
            with pe.Fori(0, NC) as c:
                cols = bass.ds(c * CH, CH)
                for p in range(NP + 1):
                    if p < NP:
                        if p >= 2:
                            pe.wait_ge(weighted, c * NP + (p - 1))
                        pe.matmul(ps_g[p % 2][:, :], Wg[:, p, :], xn[:, cols], start=True, stop=True)
                        last = pe.matmul(ps_u[p % 2][:, :], Wu[:, p, :], xn[:, cols], start=True, stop=True)
                        if p < NP - 1:
                            last = pe.matmul(ps_w[p % 2][:, :], pick[:, p, :], comb[:, cols], start=True, stop=True)
                        last.then_inc(made, 1)
                    if p >= 1:
                        k = p - 1
                        if k == 0:
                            pe.wait_ge(joined, c + 1)
                        pe.wait_ge(weighted, c * NP + (k + 1))
                        last = pe.matmul(ps_o[:, :], Wd[:, k, :], prod[k % 2][:, :], start=(k == 0), stop=(k == NP - 1))
                last.then_inc(summed, 1)

        @block.scalar
        def _(act):
            with act.Fori(0, NC) as c:
                for p in range(NP):
                    act.wait_ge(made, c * NP + (p + 1))
                    act.activation(act_g[p % 2][:, :], ps_g[p % 2][:, :], ACT.Silu).then_inc(gated, 1)

        @block.vector
        def _(dve):
            dve.sem_inc(joined, 1)
            with dve.Fori(0, NC) as c:
                for p in range(NP):
                    dve.wait_ge(gated, c * NP + (p + 1))
                    if p < NP - 1:
                        dve.tensor_tensor(act_g[p % 2][:, :], act_g[p % 2][:, :], ps_u[p % 2][:, :], ALU.mult)\
                           .then_inc(multiplied, 1)
                        dve.wait_ge(multiplied, c * (NP - 1) + (p + 1))
                        dve.tensor_tensor(prod[p % 2][:, :], act_g[p % 2][:, :], ps_w[p % 2][:, :], ALU.mult).then_inc(weighted, 1)
                    else:
                        dve.tensor_tensor(prod[p % 2][:, :], act_g[p % 2][:, :], ps_u[p % 2][:, :], ALU.mult)\
                           .then_inc(weighted, 1)
                dve.wait_ge(summed, c + 1)
                cols = bass.ds(c * CH, CH)
                dve.tensor_tensor(S.hT[:, cols], S.hT[:, cols], ps_o[:, :], ALU.add).then_inc(joined, 1)

    with stage(nc) as ctx:
        block = ctx.enter_context(nc.Block())

        @block.vector
        def _(dve):
            for b in range(B):
                dve.scalar_tensor_tensor(out=S.xT[:, batch(b)], in0=S.hT[:, batch(b)], scalar=S.mod[:, 0, 5, b:b + 1],
                                         in1=S.xT[:, batch(b)], op0=ALU.mult, op1=ALU.add)


def full_experts(nc, S, A, comb):
    NC, R, F = N // CH, X + 1, 4
    READ = 2
    I32 = mybir.dt.int32
    with ExitStack() as outer:
        y = outer.enter_context(nc.sbuf_tensor("f_y", [D, N], F32))
        with stage(nc) as ctx:
            def sb(name, shape, dt=F32):
                return ctx.enter_context(nc.sbuf_tensor("f_" + name, shape, dt))

            def sem(name):
                return semaphore(nc, ctx, "f_" + name)

            W1, W2 = sb("W1", [D, R, F, 128]), sb("W2", [128, R, F, D])
            pick = sb("pick", [R, R, 128])
            most, used_by, used = sb("most", [R, NC]), sb("used_by", [R, NC], I32), sb("used", [1, R * NC], I32)
            hidden = [sb(f"hidden{i}", [128, F, CH]) for i in range(2)]
            biased = [sb(f"biased{i}", [D, CH]) for i in range(2)]
            part = sb("part", [D, CH])
            ps_h = [ctx.enter_context(nc.psum_tensor(f"f_ps_h{i}", [128, 2, CH], F32)) for i in range(2)]
            ps_y = [ctx.enter_context(nc.psum_tensor(f"f_ps_y{i}", [128, CH], F32)) for i in range(2)]
            ps_w = [ctx.enter_context(nc.psum_tensor(f"f_ps_w{i}", [128, CH], F32)) for i in range(2)]
            loaded, up, gelu, down, offset, weighted, chain = [sem(x) for x in ("loaded", "up", "gelu", "down", "offset", "weighted", "chain")]
            flagged, flags_ready = sem("flagged"), sem("flags_ready")
            block = ctx.enter_context(nc.Block())

            def is_used(eng, c, e):
                return eng.value_load(used[0:1, bass.ds(c + e * NC, 1)], min_val=0, max_val=1) > 0

            @block.sync
            def _(sp):
                sp.dma_start(pick[:, :, :], A["pick_r"].rearrange("e (n p) -> e n p", p=128)).then_inc(loaded, 16)
                for e in range(X):
                    sp.dma_start(W1[:, e, :, :].rearrange("d f i -> d (f i)"), A["W1"][e]).then_inc(loaded, 16)
                    sp.dma_start(W2[:, e, :, :], A["W2"][e].rearrange("(f i) d -> i f d", i=128)).then_inc(loaded, 16)
                sp.dma_start(W1[:, X, :, :].rearrange("d f i -> d (f i)"), A["fw1"]).then_inc(loaded, 16)
                sp.dma_start(W2[:, X, :, :], A["fw2"].rearrange("(f i) d -> i f d", i=128)).then_inc(loaded, 16)

            @block.gpsimd
            def _(pool):
                pool.wait_ge(flagged, 2)
                for e in range(R):
                    pool.dma_start(used[0:1, e * NC:(e + 1) * NC], used_by[e:e + 1, :]).then_inc(flags_ready, 16)

            @block.tensor
            def _(pe):
                pe.wait_ge(flags_ready, 16 * R)
                pe.wait_ge(loaded, 16 * (2 * R + 1))
                with pe.Fori(0, NC) as c:
                    cols = bass.ds(c * CH, CH)
                    for e in range(R):
                        with pe.If(is_used(pe, c, e)):
                            for half in range(2):
                                for f in range(2):
                                    last = pe.matmul(ps_h[half][:, f, :], W1[:, e, 2 * half + f, :], S.hT[:, cols], start=True, stop=True)
                                last.then_inc(up, 1)
                            pe.wait_ge(weighted, c * R + (max(0, e - 1) + READ))
                            pe.matmul(ps_w[e % 2][:, :], pick[:, e, :], comb[:, cols], start=True, stop=True)
                            for f in range(F):
                                pe.wait_ge(gelu, c * (4 * R) + (4 * e + f + 1))
                                last = pe.matmul(ps_y[e % 2][:, :], W2[:, e, f, :], hidden[e % 2][:, f, :], start=(f == 0), stop=(f == F - 1))
                            last.then_inc(down, 1)
                        with pe.Else():
                            pe.drain()
                            pe.sem_inc(up, 2)
                            pe.sem_inc(down, 1)

            @block.scalar
            def _(act):
                act.wait_ge(flags_ready, 16 * R)
                with act.Fori(0, NC) as c:
                    for e in range(R):
                        with act.If(is_used(act, c, e)):
                            for half in range(2):
                                act.wait_ge(up, c * (2 * R) + (2 * e + half + 1))
                                for f in range(2):
                                    bias = S.vec("b1", 4 * e + 2 * half + f) if e < X else S.vec("fb1", 2 * half + f)
                                    act.activation(hidden[e % 2][:, 2 * half + f, :], ps_h[half][:, f, :], ACT.Gelu, bias=bias)\
                                       .then_inc(gelu, 1)
                            act.wait_ge(down, c * R + (e + 1))
                            act.activation(biased[e % 2][:, :], ps_y[e % 2][:, :], ACT.Identity,
                                           bias=S.vec("b2", e) if e < X else S.vec("fb2")).then_inc(offset, 1)
                        with act.Else():
                            act.drain()
                            act.sem_inc(gelu, 4)
                            act.sem_inc(offset, 1)

            @block.vector
            def _(dve):
                dve.sem_inc(weighted, READ)
                dve.memset(y[:, :], 0.0).then_inc(chain, 1)
                dve.tensor_reduce(most[:, :], comb[:, :].rearrange("r (c t) -> r c t", t=CH), AX.X, ALU.max).then_inc(flagged, 1)
                dve.wait_ge(flagged, 1)
                dve.tensor_scalar(used_by[:, :], most[:, :], 0.0, None, ALU.is_gt).then_inc(flagged, 1)
                dve.wait_ge(flags_ready, 16 * R)
                with dve.Fori(0, NC) as c:
                    to = y[:, bass.ds(c * CH, CH)]
                    for e in range(R):
                        with dve.If(is_used(dve, c, e)):
                            dve.wait_ge(offset, c * R + (e + 1))
                            dve.wait_ge(chain, c * R + (e + 1))
                            dve.tensor_tensor(part[:, :], biased[e % 2][:, :], ps_w[e % 2][:, :], ALU.mult).then_inc(weighted, 1)
                            dve.wait_ge(weighted, c * R + (e + 1 + READ))
                            dve.tensor_tensor(to, to, part[:, :], ALU.add).then_inc(chain, 1)
                        with dve.Else():
                            dve.drain()
                            dve.sem_inc(weighted, 1)
                            dve.sem_inc(chain, 1)

        block = outer.enter_context(nc.Block())

        @block.vector
        def _(dve):
            for b in range(B):
                dve.scalar_tensor_tensor(out=S.xT[:, batch(b)], in0=y[:, batch(b)], scalar=S.mod[:, 1, 5, b:b + 1],
                                         in1=S.xT[:, batch(b)], op0=ALU.mult, op1=ALU.add)


def program(nc, A):
    S = State()
    with ExitStack() as ctx:
        S.xT = ctx.enter_context(nc.sbuf_tensor("xT_sb", [D, N], F32))
        S.hT = ctx.enter_context(nc.sbuf_tensor("hT", [D, N], F32))
        S.vecs = ctx.enter_context(nc.sbuf_tensor("vecs_sb", [D, NVEC], F32))
        S.mod = ctx.enter_context(nc.sbuf_tensor("mod", [D, 2, 6, B], F32))
        S.mean = ctx.enter_context(nc.sbuf_tensor("mean_mat", [D, D], F32))
        S.mean_sel = ctx.enter_context(nc.sbuf_tensor("mean_sel_sb", [D, N // CH, D], F32))
        S.spread = ctx.enter_context(nc.sbuf_tensor("spread_sb", [D, N // CH, D], F32))
        S.ident = ctx.enter_context(nc.sbuf_tensor("ident_sb", [D, D], F32))
        S.ident_bf = ctx.enter_context(nc.sbuf_tensor("ident_bf", [D, D], BF16))
        S.eps = ctx.enter_context(nc.sbuf_tensor("eps", [D, 1], F32))
        with nc.Block() as block:
            @block.gpsimd
            def _(pool):
                pool.memset(S.eps[:, :], LN_EPS)
        setup(nc, S, A)
        layernorm(nc, S, 0, 0)
        recurrent(nc, S, A)
        layernorm(nc, S, 0, 1)
        latent_attention(nc, S, A)
        with ExitStack() as half:
            xn = half.enter_context(nc.sbuf_tensor("xn_moe", [D, N], F32))
            comb = half.enter_context(nc.sbuf_tensor("comb0", [X, N], F32))
            rmsnorm(nc, S, S.hT, xn, "ln2", "rms2")
            route(nc, S, A, 0, xn, comb)
            gated_experts(nc, S, A, xn, comb)
        layernorm(nc, S, 1, 0)
        head_attention(nc, S, A)
        layernorm(nc, S, 1, 1)
        with ExitStack() as half:
            comb = half.enter_context(nc.sbuf_tensor("comb1", [X + 1, N], F32))
            route(nc, S, A, 1, S.hT, comb)
            full_experts(nc, S, A, comb)
        store(nc, S, A)


def store(nc, S, A):
    with stage(nc) as ctx:
        stored = semaphore(nc, ctx, "stored")
        block = ctx.enter_context(nc.Block())

        @block.sync
        def _(sp):
            for b in range(B):
                sp.dma_start(A["out"][:, batch(b)], S.xT[:, batch(b)]).then_inc(stored, 16)
            sp.wait_ge(stored, 16 * B)


def layout(i):
    def cols(a):
        return a.reshape(-1, 128).T

    def swapped(a):
        return a.reshape(*a.shape[:-1], -1, 2)[..., ::-1].reshape(a.shape)

    def grouped(a, lo, hi):
        return a.reshape(a.shape[0], H, -1)[:, :, lo:hi].reshape(a.shape[0], -1)

    v = {
        "b_in": cols(i["L0_attn_b_in"]),
        "conv_w": i["L0_attn_conv_w"].reshape(2, 128, 4).transpose(1, 0, 2).reshape(128, 8),
        "conv_b": cols(i["L0_attn_conv_b"]), "Dp": cols(i["L0_attn_Dp"]), "b_out": cols(i["L0_attn_b_out"]),
        "ln1": cols(i["L0_ffn_w_ln1"]), "ln2": cols(i["L0_ffn_w_ln2"]),
        "Wu_q_b": cols(i["L1_attn_Wu_q_b"]), "Wq_r_b": cols(i["L1_attn_Wq_r_b"]), "Wq_r_bs": cols(swapped(i["L1_attn_Wq_r_b"])),
        "Wk_r_b": cols(i["L1_attn_Wk_r_b"]), "Wk_r_bs": cols(swapped(i["L1_attn_Wk_r_b"])), "Wu_k_b": cols(i["L1_attn_Wu_k_b"]),
        "Wo_b": cols(i["L1_attn_Wo_b"]), "b1": cols(i["L1_ffn_b1"]), "b2": cols(i["L1_ffn_b2"]),
        "fb1": cols(i["L1_ffn_fb1"]), "fb2": cols(i["L1_ffn_fb2"]),
    }
    Wq, Wkva = i["L0_ffn_Wq"], i["L0_ffn_Wkva"]
    a = {
        "xT": i["L0_attn_x"].reshape(N, D).T, "c0T": i["L0_c"].T, "c1T": i["L1_c"].T,
        "wmod0": i["L0_wmod"], "wmod1": i["L1_wmod"],
        "vecs": np.concatenate([v[n] for n in VEC], axis=1),
        "W_in": i["L0_attn_W_in"], "A": i["L0_attn_A"], "CT": i["L0_attn_C"].T, "W_out": i["L0_attn_W_out"],
        "Wq_n": grouped(Wq, 0, 32), "Wq_r": grouped(Wq, 32, 64), "Wq_rs": swapped(grouped(Wq, 32, 64)),
        "Wkv_l": Wkva[:, 0:16], "Wk_r0": Wkva[:, 16:48], "Wk_r0s": swapped(Wkva[:, 16:48]), "Wkvb": i["L0_ffn_Wkvb"],
        "Wo0": i["L0_ffn_Wo"].reshape(H, 64, D)[:, 0:32].reshape(H * 32, D),
        "Wgate": i["L0_ffn_Wgate"], "gate_b": i["L0_ffn_expert_bias"].reshape(1, 8),
        "Wg": i["L0_ffn_Wg"], "Wu": i["L0_ffn_Wu"], "Wd": i["L0_ffn_Wd"],
        "sWg": i["L0_ffn_sWg"], "sWu": i["L0_ffn_sWu"], "sWd": i["L0_ffn_sWd"],
        "Wd_q": i["L1_attn_Wd_q_w"], "Wd_kv": i["L1_attn_Wd_kv_w"], "bd_q": i["L1_attn_Wd_q_b"].reshape(64, 1),
        "bd_kv": i["L1_attn_Wd_kv_b"].reshape(64, 1), "Wu_q": i["L1_attn_Wu_q_w"], "Wq_r1": i["L1_attn_Wq_r_w"],
        "Wq_r1s": swapped(i["L1_attn_Wq_r_w"]), "Wk_r1": i["L1_attn_Wk_r_w"], "Wk_r1s": swapped(i["L1_attn_Wk_r_w"]),
        "Wu_k": i["L1_attn_Wu_k_w"], "Wu_v": i["L1_attn_Wu_v_w"], "bu_v": i["L1_attn_Wu_v_b"].reshape(1, D),
        "Wo1": i["L1_attn_Wo_w"], "Wr": i["L1_ffn_Wr"], "W1": i["L1_ffn_W1"], "W2": i["L1_ffn_W2"],
        "fw1": i["L1_ffn_fw1"], "fw2": i["L1_ffn_fw2"],
    }
    a = {n: np.ascontiguousarray(x) for n, x in a.items()}
    a.update(constants())
    return a


def constants():
    t = np.arange(T, dtype=np.float32)
    f0 = (1.0 / np.float32(100000.0) ** (np.arange(0, 32, 2, dtype=np.float32) / np.float32(32))).astype(np.float32)
    a0 = np.outer(t, f0).astype(np.float32)
    f1 = (np.float32(10000.0) ** (np.float32(-2.0) * np.arange(64, dtype=np.float32)) / np.float32(64)).astype(np.float32)
    a1 = (t[:, None] * f1[None, :]).astype(np.float32)
    sign = np.tile(np.array([-1.0, 1.0], np.float32), 64)[:, None]

    def rows(x):
        x = np.repeat(x.T, 2, axis=0)
        return np.tile(x, (128 // x.shape[0], 1)).astype(np.float32)

    q = np.arange(128)
    j = np.arange(HG)
    head = np.arange(H)
    c = {
        "sel0": (q[:, None] // 3 == j[None, :]), "sel1": ((q[:, None] - 96) // 3 == j[None, :]),
        "pick0": (np.arange(H * 32)[None, :] // 32 == head[:, None]), "pick1": (q[None, :] // 8 == head[:, None]),
        "pick_e": (np.arange(X * 64)[None, :] // 64 == np.arange(X)[:, None]),
        "pick_r": (np.arange((X + 1) * 128)[None, :] // 128 == np.arange(X + 1)[:, None]),
        "number": np.arange(X)[None, :], "before": (q[:, None] < q[None, :]),
        "mean_sel": (np.arange(8 * 128)[None, :] == 129 * (np.arange(8 * 128)[None, :] // 128)) / np.float32(D) * np.ones((D, 1)),
        "spread": (np.arange(8 * 128)[None, :] // 128 == q[:, None]),
        "ident": np.eye(128, dtype=np.float32),
        "cos0": rows(np.cos(a0)), "sin0": rows(np.sin(a0)) * sign,
        "cos1": rows(np.cos(a1)), "sin1": rows(np.sin(a1)) * sign,
        "mask": np.where(q[:, None] >= q[None, :], 0.0, NEG).astype(np.float32),
        "maskT": np.where(q[:, None] <= q[None, :], 0.0, NEG).astype(np.float32),
    }
    return {n: np.ascontiguousarray(x, dtype=np.float32) for n, x in c.items()}


def kernel(**inputs):
    from concourse import bacc
    from concourse.bass_utils import run_bass_kernel_spmd

    nc = bacc.Bacc("TRN2", target_bir_lowering=False, num_devices=1)
    arrays, A = {}, {}
    for name, a in layout(inputs).items():
        arrays["in_" + name] = a
        A[name] = nc.dram_tensor("in_" + name, a.shape, mybir.dt.from_np(a.dtype), kind="ExternalInput").ap()
    A["out"] = nc.dram_tensor("out_xT", (D, N), F32, kind="ExternalOutput").ap()
    program(nc, A)
    r = run_bass_kernel_spmd(nc, [arrays], core_ids=[0])
    return np.asarray(r.results[0]["out_xT"]).T.reshape(B, T, D)
```
